# Optimizing a Trainium2 kernel written in Bass

```python
import numpy as np
import jax
import jax.numpy as jnp

def _softmax(x, axis=-1):
    return jax.nn.softmax(x, axis=axis)

def _gelu(x):
    return jax.nn.gelu(x, approximate=True)

def _silu(x):
    return jax.nn.silu(x)

def _sigmoid(x):
    return jax.nn.sigmoid(x)

def _layernorm(x, axis=-1, eps=1e-05):
    m = jnp.mean(x, axis=axis, keepdims=True)
    v = jnp.var(x, axis=axis, keepdims=True)
    return (x - m) / jnp.sqrt(v + eps)

def _scatter_add(tgt, idx, src, axis=0):
    return tgt.at[idx].add(src)

def _segment_sum(src, seg, n):
    return jax.ops.segment_sum(src, seg, n)
kernel_name = 'mk_adj_resnorm_d1_adj_r2_0bd230'

def setup_inputs(seed: int=0):
    np.random.seed(seed)
    _w = jnp.asarray

    def _rec_inputs():
        import jax
        import jax.numpy as jnp
        _gk = jax.random.key(seed)
        x = 0.0002141 + 1 * jax.random.normal(jax.random.fold_in(_gk, 1), (128, 64, 384), jnp.float32)
        _a = jax.random.bernoulli(jax.random.fold_in(_gk, 2), 0.0625, (128, 64, 64))
        _a = jnp.logical_or(_a, jnp.swapaxes(_a, -1, -2))
        _a = jnp.logical_or(_a, jnp.eye(64, dtype=bool))
        adj = _a.astype(jnp.int32)
        return (x, adj)
    x, adj = _rec_inputs()

    def _L0_gnn_setup():
        import jax, jax.numpy as jnp
        import numpy as np
        B, S, HID, DEP, DS, NTYPES = (8, 128, 384, 64, 384, 45)
        NEG = -1000000000.0
        key = jax.random.key(seed)
        ks = jax.random.split(key, 10)
        sc = lambda fan_in: 1.0 / np.sqrt(fan_in)
        return {'h': jax.random.normal(ks[0], (B, S, HID), dtype=jnp.float32), 'dep_type_matrix': jax.random.randint(ks[1], (B, S, S), 0, NTYPES), 'dep_emb_table': jax.random.normal(ks[2], (NTYPES, DEP), dtype=jnp.float32), 'W1_w': jax.random.normal(ks[3], (HID + DEP, DS), dtype=jnp.float32) * sc(HID + DEP), 'W1_b': jnp.zeros((DS,), dtype=jnp.float32), 'W2_w': jax.random.normal(ks[4], (HID + DEP, DS), dtype=jnp.float32) * sc(HID + DEP), 'W2_b': jnp.zeros((DS,), dtype=jnp.float32), 'gcn_w': jax.random.normal(ks[5], (HID, HID), dtype=jnp.float32) * sc(HID), 'gcn_b': jnp.zeros((HID,), dtype=jnp.float32), 'Wo_w': jax.random.normal(ks[6], (DS, HID), dtype=jnp.float32) * sc(DS), 'Wo_b': jnp.zeros((HID,), dtype=jnp.float32)}
    _L0_gnn_all = _L0_gnn_setup()
    _L0_gnn_in = {k: v for k, v in _L0_gnn_all.items() if k in ('dep_emb_table', 'W1_w', 'W1_b', 'W2_w', 'W2_b', 'gcn_w', 'gcn_b', 'Wo_w', 'Wo_b')}
    del _L0_gnn_all
    return {'x': x, 'adj': adj, 'L0_gnn_dep_emb_table': _L0_gnn_in['dep_emb_table'], 'L0_gnn_W1_w': _L0_gnn_in['W1_w'], 'L0_gnn_W1_b': _L0_gnn_in['W1_b'], 'L0_gnn_W2_w': _L0_gnn_in['W2_w'], 'L0_gnn_W2_b': _L0_gnn_in['W2_b'], 'L0_gnn_gcn_w': _L0_gnn_in['gcn_w'], 'L0_gnn_gcn_b': _L0_gnn_in['gcn_b'], 'L0_gnn_Wo_w': _L0_gnn_in['Wo_w'], 'L0_gnn_Wo_b': _L0_gnn_in['Wo_b']}

def reference(x, adj, L0_gnn_dep_emb_table, L0_gnn_W1_w, L0_gnn_W1_b, L0_gnn_W2_w, L0_gnn_W2_b, L0_gnn_gcn_w, L0_gnn_gcn_b, L0_gnn_Wo_w, L0_gnn_Wo_b):
    import jax
    import jax.numpy as jnp

    def _L0_gnn_ref(h, dep_type_matrix, dep_emb_table, W1_w, W1_b, W2_w, W2_b, gcn_w, gcn_b, Wo_w, Wo_b):
        import jax, jax.numpy as jnp
        import numpy as np
        B, S, HID, DEP, DS, NTYPES = (8, 128, 384, 64, 384, 45)
        NEG = -1000000000.0
        adj = dep_type_matrix != 0
        dep_emb = dep_emb_table[dep_type_matrix]
        hi_t = jnp.einsum('bid,de->bie', h, W1_w[:HID])[:, :, None, :] + jnp.einsum('bijd,de->bije', dep_emb, W1_w[HID:]) + W1_b
        hj_t = jnp.einsum('bjd,de->bje', h, W2_w[:HID])[:, None, :, :] + jnp.einsum('bijd,de->bije', dep_emb, W2_w[HID:]) + W2_b
        relevance = jnp.sum(hi_t * hj_t, axis=-1)
        masked = jnp.where(adj, relevance, NEG)
        A = jax.nn.softmax(masked, axis=2)
        h_syn = h
        for _ in range(1):
            aggregated = jnp.einsum('bij,bjd->bid', A, h_syn)
            h_syn = jax.nn.relu(aggregated @ gcn_w + gcn_b)
        return h_syn @ Wo_w + Wo_b
    x = _layernorm(x + _L0_gnn_ref(x, adj, L0_gnn_dep_emb_table, L0_gnn_W1_w, L0_gnn_W1_b, L0_gnn_W2_w, L0_gnn_W2_b, L0_gnn_gcn_w, L0_gnn_gcn_b, L0_gnn_Wo_w, L0_gnn_Wo_b), axis=-1)
    return x

_drawn_inputs = setup_inputs


def setup_inputs(seed=0):
    import zlib

    import numpy as np

    out = dict(_drawn_inputs(seed))
    spreads = {'L0_gnn_W1_b': (0.0, 0.1),
     'L0_gnn_W2_b': (0.0, 0.1),
     'L0_gnn_gcn_b': (0.0, 0.1),
     'L0_gnn_Wo_b': (0.0, 0.1)}
    factors = {}
    for name, (base, spread) in spreads.items():
        noise = np.random.default_rng([zlib.crc32(name.encode()), seed]).standard_normal(out[name].shape)
        drawn = base * np.exp(spread * noise) if base else spread * noise
        out[name] = jnp.asarray(drawn.astype(out[name].dtype))
    for name, factor in factors.items():
        out[name] = (out[name] * factor).astype(out[name].dtype)
    return out
```

```python
from contextlib import ExitStack

import numpy as np

import concourse.bass as bass
from concourse import mybir

F32 = mybir.dt.float32
F32R = mybir.dt.float32r
I32 = mybir.dt.int32
ALU = mybir.AluOpType
ACT = mybir.ActivationFunctionType
AX = mybir.AxisListType
ds = bass.ds

P = 128
NEG = -1.0e9
EPS = 1.0e-5


def build(nc, x, adj, emb, w1, b1, w2, b2, gcn_w, gcn_b, wo, wo_b, out):
    NGRAPH, S, D = x.shape
    NT, DEP = emb.shape
    K = D // P
    R = NGRAPH * S
    TILES = R // P
    H = P // S
    T = 4
    GROUPS = TILES // T
    GW = T * P
    XC = D + 2
    assert H == 2 and GW == 512 and GROUPS % 2 == 0 and S == 64

    x_rows = x.rearrange("b s d -> (b s) d")
    x_groups = x_rows.rearrange("(g t p) d -> g p t d", t=T, p=P)
    x_tiles = x_rows.rearrange("(k p) d -> k p d", p=P)
    out_groups = out.rearrange("b s d -> (b s) d").rearrange("(g t p) d -> g p t d", t=T, p=P)
    adj_tiles = adj.rearrange("b s j -> (b s) j").rearrange("(k p) j -> p k j", p=P)
    chunked = lambda m: m.rearrange("(k p) e -> p k e", p=P)
    column = lambda v: v.rearrange("(k p) -> p k", p=P)
    row_on_all = lambda v: v.rearrange("(a n) -> a n", a=1).broadcast_to((P, D))

    q_scratch = nc.dram_tensor("q_scratch", (P, NT), F32, kind="Internal").ap()

    ctx = ExitStack()
    with ctx:
        sb = lambda name, shape, dt=F32: ctx.enter_context(nc.sbuf_tensor(name, shape, dt))
        sem = lambda name: ctx.enter_context(nc.semaphore(name))
        bank = lambda name: ctx.enter_context(nc.psum_tensor(name, [P, 512], F32))

        ident = sb("ident", [P, P])
        ones = sb("ones", [P, P])
        half = sb("half", [P, 1])
        minus_half = sb("minus_half", [P, T])
        minus_one = sb("minus_one", [P, T])
        w1_d = sb("w1_d", [P, K, D])
        w2_d = sb("w2_d", [P, K, D])
        w1_e = sb("w1_e", [P, K, D])
        w2_e = sb("w2_e", [P, K, D])
        w1_dep = sb("w1_dep", [DEP, D])
        w2_dep = sb("w2_dep", [DEP, D])
        emb1 = sb("emb1", [DEP, 1])
        b1_col = sb("b1_col", [P, K])
        b2_col = sb("b2_col", [P, K])
        b1p = sb("b1p", [P, K])
        b2p = sb("b2p", [P, K])
        b1b2 = sb("b1b2", [P, K])
        u_col = sb("u_col", [P, K])
        gcn_raw = sb("gcn_raw", [P, K, D])
        wo_raw = sb("wo_raw", [P, K, D])
        g_hi = sb("g_hi", [P, K, D], F32R)
        g_lo = sb("g_lo", [P, K, D], F32R)
        gw_hi = sb("gw_hi", [P, K, XC], F32R)
        gw_lo = sb("gw_lo", [P, K, XC], F32R)
        wo_hi = sb("wo_hi", [P, K, D], F32R)
        wo_lo = sb("wo_lo", [P, K, D], F32R)
        xw_bias = sb("xw_bias", [P, D + 1])
        wo_bias = sb("wo_bias", [P, D])
        flag_part = sb("flag_part", [P, 1])
        flag = sb("flag", [1, 1], I32)

        adj_sb = sb("adj_sb", [P, TILES, S], I32)
        bias_sb = sb("bias_sb", [P, TILES, S])

        x_in = sb("x_in", [P, 2, T, D])
        x_res = sb("x_res", [P, 2, T, D])
        xT = sb("xT", [P, K, GW])
        xT_hi = sb("xT_hi", [P, K, GW], F32R)
        xT_lo = sb("xT_lo", [P, K, GW], F32R)
        yT = sb("yT", [P, K, GW])
        xw = sb("xw", [P, T, XC])
        score = sb("score", [P, T, S])
        row_max = sb("row_max", [P, T])
        prob = sb("prob", [P, T, S])
        row_sum = sb("row_sum", [P, T])
        inv_sum = sb("inv_sum", [P, 2, T])
        probT = sb("probT", [P, T, P])
        h_hi = sb("h_hi", [P, K, GW], F32R)
        h_lo = sb("h_lo", [P, K, GW], F32R)
        y = sb("y", [P, 2, T, D])
        stats = sb("stats", [P, T, 6])
        mean_var = sb("mean_var", [P, 2, T, 2])
        var_eps = sb("var_eps", [P, T])
        rstd = sb("rstd", [P, 2, T])
        mean_rstd = sb("mean_rstd", [P, T])
        shift = sb("shift", [P, 2, T])

        embT = sb("embT", [DEP, NT])
        d1T = sb("d1T", [P, K, NT])
        d2T = sb("d2T", [P, K, NT])
        d2b = sb("d2b", [P, K, NT])
        dd = sb("dd", [P, K, NT])
        uv = sb("uv", [P, K, 2 * NT])
        pq_row = sb("pq_row", [1, 2 * NT])
        xg = sb("xg", [P, D])
        xgT = sb("xgT", [P, K, P])
        pq = sb("pq", [P, 2 * NT])
        q_all = sb("q_all", [P, S, NT])
        onehot = sb("onehot", [P, S, NT])
        type_iota = sb("type_iota", [P, NT])
        kind = sb("kind", [P, S])
        wrapped = sb("wrapped", [P, S])
        extra = sb("extra", [P, S])

        wide = [bank(f"wide{c}") for c in range(K)]
        turn = [bank(f"turn{n}") for n in range(3)]
        ps_score = bank("ps_score")
        ps_probT = bank("ps_probT")
        xw_bank = lambda t: turn[t % 3]
        xT_bank = lambda t: turn[(T + t) % 3]
        out_bank = lambda t: turn[(2 * T + t) % 3]

        w1_loaded, w2_loaded, dep_loaded, gcn_loaded, wo_loaded, adj_loaded, bias_loaded = (
            sem(n + "_loaded") for n in ("w1", "w2", "dep", "gcn", "wo", "adj", "bias"))
        x_loaded = [sem(f"x_loaded{s}") for s in range(2)]
        out_stored = [sem(f"out_stored{s}") for s in range(2)]
        const_ready = sem("const_ready")
        turned_w = sem("turned_w")
        w_e_act = sem("w_e_act")
        w_e_dve = sem("w_e_dve")
        dep_done = sem("dep_done")
        bp_ready = sem("bp_ready")
        g_done = sem("g_done")
        g_hi_ready = sem("g_hi_ready")
        g_lo_ready = sem("g_lo_ready")
        uw_done = sem("uw_done")
        u_ready = sem("u_ready")
        split_hi = sem("split_hi")
        weights_ready = sem("weights_ready")
        zeroed = sem("zeroed")
        squared = sem("squared")
        flag_sum = sem("flag_sum")
        flag_ready = sem("flag_ready")
        bias_ready = sem("bias_ready")
        xT_done = sem("xT_done")
        xT_hi_ready = sem("xT_hi_ready")
        xT_lo_ready = sem("xT_lo_ready")
        x_res_ready = sem("x_res_ready")
        y_done = sem("y_done")
        yT_ready = sem("yT_ready")
        xw_done = sem("xw_done")
        xw_ready = sem("xw_ready")
        score_done = sem("score_done")
        soft = sem("soft")
        prob_ready = sem("prob_ready")
        norm_ready = sem("norm_ready")
        probT_done = sem("probT_done")
        probT_ready = sem("probT_ready")
        agg_done = sem("agg_done")
        h_hi_ready = sem("h_hi_ready")
        h_lo_ready = sem("h_lo_ready")
        out_done = sem("out_done")
        y_ready = sem("y_ready")
        stats_ready = sem("stats_ready")
        mv_ready = sem("mv_ready")
        var_ready = sem("var_ready")
        ln_step = sem("ln_step")
        ln_ready = sem("ln_ready")
        SOFT = H + 4
        dve_held, pe_held = sem("dve_held"), sem("pe_held")
        ge_load, ge_pe, ge_act, ge_dve = sem("ge_load"), sem("ge_pe"), sem("ge_act"), sem("ge_dve")
        ge_iota = sem("ge_iota")
        GT = 10
        gt_x, gt_q, gt_qb, gt_pe, gt_act, gt_dve = (
            sem("gt_" + n) for n in ("x", "q", "qb", "pe", "act", "dve"))

        block = ctx.enter_context(nc.Block())

        def steps(eng, step):
            step(0, 0)
            step(0, 1)
            with eng.Fori(0, (GROUPS - 4) // 2) as i:
                step(i, 2)
                step(i, 3)
            step(0, GROUPS - 2)
            step(0, GROUPS - 1)

        def group(i, o):
            return 2 * i + o

        @block.sync
        def _(sp):
            sp.dma_start(w1_d[:, :, :], chunked(w1[0:D, :])).then_inc(w1_loaded, 16)
            sp.dma_start(w2_d[:, :, :], chunked(w2[0:D, :])).then_inc(w2_loaded, 16)
            sp.dma_start(x_in[:, 0, :, :], x_groups[0]).then_inc(x_loaded[0], 16)
            sp.dma_start(adj_sb[:, :, :], adj_tiles).then_inc(adj_loaded, 16)
            sp.dma_start(x_in[:, 1, :, :], x_groups[1]).then_inc(x_loaded[1], 16)
            sp.dma_start(wo_raw[:, :, :], chunked(wo)).then_inc(wo_loaded, 16)

            sp.wait_ge(flag_ready, 1)
            other_types = sp.value_load(flag[0:1, 0:1], min_val=0, max_val=1)
            with sp.If(other_types > 0):
                with sp.Fori(0, TILES) as k:
                    src = sp.snap(k)
                    sp.wait_ge(gt_dve, src * GT + 1)
                    sp.dma_start(xg[:, :], x_tiles[src]).then_inc(gt_x, 16)
                    sp.wait_ge(gt_act, src * 2 + 2)
                    sp.dma_start(q_scratch, pq[:, NT:2 * NT]).then_inc(gt_q, 16)
                    sp.wait_ge(gt_q, src * 16 + 16)
                    for h in range(H):
                        rows = q_scratch[h * S:(h + 1) * S, :].rearrange("(a s) t -> a (s t)", a=1)
                        sp.dma_start(q_all[h * S:(h + 1) * S, :, :].rearrange("p s t -> p (s t)"),
                                     rows.broadcast_to((S, S * NT))).then_inc(gt_qb, 16)

            def load(i, o):
                g = sp.snap(group(i, o))
                sp.wait_ge(xT_done, T * (g - 1))
                sp.wait_ge(x_res_ready, g - 1)
                sp.dma_start(x_in[:, o % 2, :, :], x_groups[g]).then_inc(x_loaded[o % 2], 16)

            def store(i, o):
                g = sp.snap(group(i, o))
                sp.wait_ge(ln_ready, T * (g + 1))
                sp.dma_start(out_groups[g], y[:, o % 2, :, :]).then_inc(out_stored[o % 2], 16)

            load(0, 2)
            with sp.Fori(0, (GROUPS - 4) // 2) as i:
                for o in (0, 1):
                    load(i, o + 3)
                    store(i, o)
            load(0, GROUPS - 1)
            for g in range(GROUPS - 4, GROUPS):
                store(0, g)
            sp.wait_ge(out_stored[0], 16 * GROUPS // 2)
            sp.wait_ge(out_stored[1], 16 * GROUPS // 2)

        @block.gpsimd
        def _(pool):
            pool.memset(ident[:, :], 0.0).then_inc(const_ready, 1)
            pool.wait_ge(const_ready, 1)
            pool.affine_select(out=ident[:, :], in_=ident[:, :], compare_op=ALU.not_equal, fill=1.0,
                               base=0, pattern=[[-1, P]], channel_multiplier=1).then_inc(const_ready, 1)
            pool.memset(ones[:, :], 1.0).then_inc(const_ready, 1)
            pool.memset(half[:, :], -0.5).then_inc(const_ready, 1)
            pool.memset(minus_half[:, :], -0.5).then_inc(const_ready, 1)
            pool.memset(minus_one[:, :], -1.0).then_inc(const_ready, 1)
            pool.dma_start(wo_bias[:, :], row_on_all(wo_b)).then_inc(bias_loaded, 16)
            pool.dma_start(xw_bias[:, 0:D], row_on_all(gcn_b)).then_inc(bias_loaded, 16)

            pool.wait_ge(flag_ready, 1)
            other_types = pool.value_load(flag[0:1, 0:1], min_val=0, max_val=1)
            with pool.If(other_types > 0):
                pool.dma_start(embT[:, :], emb.rearrange("t d -> d t"),
                               allow_slow_non_contiguous=True).then_inc(ge_load, 16)
                pool.iota(type_iota[:, :], pattern=[[1, NT]], base=0, channel_multiplier=0,
                          allow_small_or_imprecise_dtypes=True).then_inc(ge_iota, 1)
                pool.wait_ge(ge_load, 16)

            pool.wait_ge(bias_loaded, 32)
            pool.wait_ge(const_ready, 6)

            def residual(i, o):
                s = o % 2
                pool.wait_ge(x_loaded[s], 16 * (i + o // 2 + 1))
                if o >= 2:
                    pool.wait_ge(y_ready, T * (group(i, o) - 1))
                pool.tensor_tensor(x_res[:, s, :, :], x_in[:, s, :, :],
                                   wo_bias[:, :].unsqueeze(1).broadcast_to((P, T, D)),
                                   ALU.add).then_inc(x_res_ready, 1)

            def layer_norm(i, o):
                s, g = o % 2, group(i, o)
                pool.wait_ge(var_ready, g + 1)
                if o >= 2:
                    pool.wait_ge(ln_ready, T * (g - 1))
                mean = mean_var[:, s, :, 0]
                pool.tensor_tensor(rstd[:, s, :], var_eps[:, :], minus_half[:, :],
                                   ALU.pow).then_inc(ln_step, 1)
                pool.wait_ge(ln_step, 3 * g + 1)
                pool.tensor_tensor(mean_rstd[:, :], mean, rstd[:, s, :], ALU.mult).then_inc(ln_step, 1)
                pool.wait_ge(ln_step, 3 * g + 2)
                pool.tensor_tensor(shift[:, s, :], mean_rstd[:, :], minus_one[:, :],
                                   ALU.mult).then_inc(ln_step, 1)

            residual(0, 0)
            residual(0, 1)
            layer_norm(0, 0)
            residual(0, 2)
            layer_norm(0, 1)
            with pool.Fori(0, (GROUPS - 4) // 2) as i:
                for o in (2, 3):
                    residual(i, o + 1)
                    layer_norm(i, o)
            residual(0, GROUPS - 1)
            layer_norm(0, GROUPS - 2)
            layer_norm(0, GROUPS - 1)

        @block.scalar
        def _(act):
            act.dma_start(w1_dep[:, :], w1[D:D + DEP, :]).then_inc(dep_loaded, 16)
            act.dma_start(w2_dep[:, :], w2[D:D + DEP, :]).then_inc(dep_loaded, 16)
            act.dma_start(emb1[:, :], emb[1:2, :].rearrange("a d -> d a"),
                          allow_slow_non_contiguous=True).then_inc(dep_loaded, 16)
            act.dma_start(b1_col[:, :], column(b1), allow_slow_non_contiguous=True).then_inc(dep_loaded, 16)
            act.dma_start(b2_col[:, :], column(b2), allow_slow_non_contiguous=True).then_inc(dep_loaded, 16)
            act.dma_start(gcn_raw[:, :, :], chunked(gcn_w)).then_inc(gcn_loaded, 16)

            for c in range(K):
                act.wait_ge(turned_w, 2 * c + 1)
                act.activation(w1_e[:, c, :], wide[c][:, 0:D], ACT.Copy).then_inc(w_e_act, 1)
            for k in range(K):
                act.wait_ge(g_done, k + 1)
                act.activation(g_hi[:, k, :], turn[k][:, 0:D], ACT.Copy).then_inc(g_hi_ready, 1)
            act.wait_ge(uw_done, 1)
            act.activation(u_col[:, :], ps_score[:, 0:K], ACT.Copy).then_inc(u_ready, 1)
            act.wait_ge(gcn_loaded, 16)
            act.activation(gw_hi[:, :, 0:D], gcn_raw[:, :, :], ACT.Copy).then_inc(split_hi, 1)
            act.wait_ge(u_ready, 1)
            act.activation(gw_hi[:, :, D], ps_score[:, K:2 * K], ACT.Copy).then_inc(split_hi, 1)
            act.wait_ge(adj_loaded, 16)
            act.wait_ge(const_ready, 4)
            act.activation(bias_sb[:, :, :], adj_sb[:, :, :], ACT.Square, bias=half[:, 0:1],
                           accum_out=flag_part[:, :]).then_inc(squared, 1)
            act.wait_ge(wo_loaded, 16)
            act.activation(wo_hi[:, :, :], wo_raw[:, :, :], ACT.Copy).then_inc(split_hi, 1)

            act.wait_ge(flag_ready, 1)
            other_types = act.value_load(flag[0:1, 0:1], min_val=0, max_val=1)
            with act.If(other_types > 0):
                act.wait_ge(ge_pe, 2)
                act.activation(uv[:, :, :], ps_score[:, 0:2 * NT * K].rearrange("p (k t) -> p k t", k=K),
                               ACT.Copy).then_inc(ge_act, 1)
                act.activation(pq_row[:, :], ps_probT[0:1, 0:2 * NT], ACT.Copy).then_inc(ge_act, 1)
                with act.Fori(0, TILES) as k:
                    n = act.snap(k)
                    act.wait_ge(gt_pe, n * 2 + 1)
                    act.activation(xgT[:, :, :], wide[0][:, 0:D].rearrange("p (k r) -> p k r", k=K),
                                   ACT.Copy).then_inc(gt_act, 1)
                    act.wait_ge(gt_pe, n * 2 + 2)
                    act.activation(pq[:, :], wide[1][:, 0:2 * NT], ACT.Copy).then_inc(gt_act, 1)
                act.wait_ge(gt_act, 2 * TILES)

            def x_parts(i, o):
                g = group(i, o)
                for t in range(T):
                    act.wait_ge(xT_done, T * g + t + 1)
                    src = xT_bank(t)[:, 0:D].rearrange("p (k r) -> p k r", k=K)
                    act.activation(xT[:, :, t * P:(t + 1) * P], src, ACT.Copy)
                    act.activation(xT_hi[:, :, t * P:(t + 1) * P], src, ACT.Copy).then_inc(xT_hi_ready, 1)

            def result(i, o):
                s, g = o % 2, group(i, o)
                act.wait_ge(ln_step, 3 * g + 3)
                for t in range(T):
                    act.activation(y[:, s, t, :], y[:, s, t, :], ACT.Identity, bias=shift[:, s, t:t + 1],
                                   scale=rstd[:, s, t:t + 1]).then_inc(ln_ready, 1)

            def step(i, o):
                g = group(i, o)
                for c in range(K):
                    act.wait_ge(y_done, K * g + c + 1)
                    act.activation(yT[:, c, :], wide[c][:, :], ACT.Identity,
                                   bias=u_col[:, c:c + 1]).then_inc(yT_ready, 1)
                if o >= 2:
                    result(i, o - 2)
                if o < GROUPS - 1:
                    x_parts(i, o + 1)
                act.wait_ge(soft, SOFT * (g + 1))
                act.activation(prob[:, :, :], score[:, :, :], ACT.Exp).then_inc(prob_ready, 1)
                for c in range(K):
                    act.wait_ge(agg_done, K * g + c + 1)
                    act.activation(h_hi[:, c, :], wide[c][:, :], ACT.Relu).then_inc(h_hi_ready, 1)

            act.wait_ge(u_ready, 1)
            x_parts(0, 0)
            steps(act, step)
            result(0, GROUPS - 2)
            result(0, GROUPS - 1)

        @block.vector
        def _(dve):
            dve.memset(probT[:, :, :], 0.0).then_inc(zeroed, 1)
            dve.memset(gw_hi[:, :, D:XC].bitcast(F32), 0.0).then_inc(zeroed, 1)
            dve.memset(gw_lo[:, :, D:XC].bitcast(F32), 0.0).then_inc(zeroed, 1)
            dve.wait_ge(dep_loaded, 80)
            dve.wait_ge(dep_done, 1)
            dve.tensor_tensor(b1p[:, :], ps_probT[:, 0:K], b1_col[:, :], ALU.add).then_inc(bp_ready, 1)
            dve.tensor_tensor(b2p[:, :], ps_probT[:, K:2 * K], b2_col[:, :], ALU.add).then_inc(bp_ready, 1)
            dve.wait_ge(bp_ready, 2)
            dve.tensor_tensor(b1b2[:, :], b1p[:, :], b2p[:, :], ALU.mult).then_inc(bp_ready, 1)
            for c in range(K):
                dve.wait_ge(turned_w, 2 * c + 2)
                dve.tensor_copy(w2_e[:, c, :], turn[c][:, 0:D]).then_inc(w_e_dve, 1)
            for k in range(K):
                dve.wait_ge(g_hi_ready, k + 1)
                dve.tensor_tensor(g_lo[:, k, :], turn[k][:, 0:D], g_hi[:, k, :],
                                  ALU.subtract).then_inc(g_lo_ready, 1)
            dve.wait_ge(split_hi, 1)
            dve.tensor_tensor(gw_lo[:, :, 0:D], gcn_raw[:, :, :], gw_hi[:, :, 0:D],
                              ALU.subtract).then_inc(weights_ready, 1)
            dve.wait_ge(split_hi, 2)
            dve.wait_ge(zeroed, 3)
            dve.tensor_tensor(gw_lo[:, :, D], ps_score[:, K:2 * K], gw_hi[:, :, D],
                              ALU.subtract).then_inc(weights_ready, 1)
            dve.tensor_copy(xw_bias[:, D:D + 1], ps_score[:, 2 * K:2 * K + 1]).then_inc(weights_ready, 1)
            dve.wait_ge(flag_sum, 1)
            dve.tensor_scalar(flag[:, :], ps_probT[0:1, 2 * K:2 * K + 1], R * S / 4.0 + 1.0, None,
                              ALU.is_gt).then_inc(flag_ready, 1)
            dve.wait_ge(squared, 1)
            dve.tensor_scalar(bias_sb[:, :, :], adj_sb[:, :, :], 0.0, NEG, ALU.is_equal,
                              ALU.mult).then_inc(bias_ready, 1)
            dve.wait_ge(split_hi, 3)
            dve.tensor_tensor(wo_lo[:, :, :], wo_raw[:, :, :], wo_hi[:, :, :],
                              ALU.subtract).then_inc(weights_ready, 1)
            dve.wait_ge(bias_ready, 1)
            dve.wait_ge(weights_ready, 4)
            dve.wait_ge(bias_loaded, 32)

            dve.wait_ge(flag_ready, 1)
            other_types = dve.value_load(flag[0:1, 0:1], min_val=0, max_val=1)
            with dve.If(other_types > 0):
                dve.wait_ge(ge_pe, 1)
                for n, d in ((0, d1T), (1, d2T)):
                    e = wide[n][:, 0:K * NT].rearrange("p (k t) -> p k t", k=K)
                    dve.tensor_copy(dd[:, :, n:n + 1], e[:, :, 1:2]).then_inc(ge_dve, 1)
                    dve.wait_ge(ge_dve, 2 * n + 1)
                    dve.tensor_tensor(d[:, :, :], e, dd[:, :, n:n + 1].broadcast_to((P, K, NT)),
                                      ALU.subtract).then_inc(ge_dve, 1)
                dve.wait_ge(ge_dve, 4)
                dve.tensor_tensor(d2b[:, :, :], d2T[:, :, :],
                                  b2p[:, :].unsqueeze(2).broadcast_to((P, K, NT)),
                                  ALU.add).then_inc(ge_dve, 1)
                dve.wait_ge(ge_dve, 5)
                dve.tensor_tensor(dd[:, :, :], d1T[:, :, :], d2b[:, :, :], ALU.mult).then_inc(ge_dve, 1)
                dve.wait_ge(ge_dve, 6)
                dve.wait_ge(ge_iota, 1)
                dve.sem_inc(gt_dve, 1)
                with dve.Fori(0, TILES) as k:
                    n = dve.snap(k)
                    types = adj_sb[:, ds(n, 1), :].squeeze(1)
                    bias = bias_sb[:, ds(n, 1), :].squeeze(1)
                    wide_kind = kind[:, :].unsqueeze(2).broadcast_to((P, S, NT))
                    wide_type = type_iota[:, :].unsqueeze(1).broadcast_to((P, S, NT))
                    wide_p = pq[:, 0:NT].unsqueeze(1).broadcast_to((P, S, NT))
                    dve.tensor_scalar(wrapped[:, :], types, 0.0, float(NT), ALU.is_lt,
                                      ALU.mult).then_inc(gt_dve, 1)
                    dve.wait_ge(gt_dve, n * GT + 2)
                    dve.tensor_tensor(kind[:, :], wrapped[:, :], types, ALU.add).then_inc(gt_dve, 1)
                    dve.wait_ge(gt_dve, n * GT + 3)
                    dve.tensor_scalar(kind[:, :], kind[:, :], 0.0, float(NT - 1), ALU.max,
                                      ALU.min).then_inc(gt_dve, 1)
                    dve.wait_ge(gt_dve, n * GT + 4)
                    dve.tensor_tensor(onehot[:, :, :], wide_kind, wide_type, ALU.is_equal).then_inc(gt_dve, 1)
                    dve.wait_ge(gt_dve, n * GT + 5)
                    dve.wait_ge(gt_qb, n * 16 * H + 16 * H)
                    dve.tensor_tensor(q_all[:, :, :], q_all[:, :, :], wide_p, ALU.add).then_inc(gt_dve, 1)
                    dve.wait_ge(gt_dve, n * GT + 6)
                    dve.tensor_tensor(onehot[:, :, :], onehot[:, :, :], q_all[:, :, :],
                                      ALU.mult).then_inc(gt_dve, 1)
                    dve.wait_ge(gt_dve, n * GT + 7)
                    dve.tensor_reduce(extra[:, :], onehot[:, :, :], AX.X, ALU.add).then_inc(gt_dve, 1)
                    dve.tensor_scalar(wrapped[:, :], types, 0.0, None, ALU.not_equal).then_inc(gt_dve, 1)
                    dve.wait_ge(gt_dve, n * GT + 9)
                    dve.tensor_tensor(extra[:, :], extra[:, :], wrapped[:, :], ALU.mult).then_inc(gt_dve, 1)
                    dve.wait_ge(gt_dve, n * GT + 10)
                    dve.tensor_tensor(bias, bias, extra[:, :], ALU.add).then_inc(gt_dve, 1)
                    dve.wait_ge(gt_dve, n * GT + 11)

            def x_low(i, o, t):
                dve.wait_ge(xT_hi_ready, T * group(i, o) + t + 1)
                cols = slice(t * P, (t + 1) * P)
                dve.tensor_tensor(xT_lo[:, :, cols], xT[:, :, cols], xT_hi[:, :, cols],
                                  ALU.subtract).then_inc(xT_lo_ready, 1)

            def softmax_scores(i, o):
                g = group(i, o)
                dve.wait_ge(score_done, g + 1)
                if o >= 1:
                    dve.wait_ge(prob_ready, g)
                for h in range(H):
                    rows = slice(h * S, (h + 1) * S)
                    src = ps_score[rows, :].rearrange("p (t r) -> p t r", t=T)[:, :, rows]
                    dve.tensor_tensor(score[rows, :, :], src,
                                      xw[rows, :, D:D + 1].broadcast_to((S, T, S)),
                                      ALU.add).then_inc(soft, 1)
                dve.wait_ge(soft, SOFT * g + H)
                dve.scalar_tensor_tensor(out=score[:, :, :], in0=adj_sb[:, ds(T * g, T), :], scalar=0.0,
                                         in1=score[:, :, :], op0=ALU.not_equal,
                                         op1=ALU.mult).then_inc(soft, 1)
                dve.wait_ge(soft, SOFT * g + H + 1)
                dve.tensor_tensor(score[:, :, :], score[:, :, :], bias_sb[:, ds(T * g, T), :],
                                  ALU.add).then_inc(soft, 1)
                dve.wait_ge(soft, SOFT * g + H + 2)
                dve.tensor_reduce(row_max[:, :], score[:, :, :], AX.X, ALU.max).then_inc(soft, 1)
                dve.wait_ge(soft, SOFT * g + H + 3)
                dve.tensor_tensor(score[:, :, :], score[:, :, :],
                                  row_max[:, :].unsqueeze(2).broadcast_to((P, T, S)),
                                  ALU.subtract).then_inc(soft, 1)

            def softmax_sums(i, o):
                g = group(i, o)
                dve.wait_ge(prob_ready, g + 1)
                dve.tensor_reduce(row_sum[:, :], prob[:, :, :], AX.X, ALU.add).then_inc(norm_ready, 1)
                dve.wait_ge(norm_ready, 2 * g + 1)
                dve.reciprocal(inv_sum[:, o % 2, :], row_sum[:, :]).then_inc(norm_ready, 1)

            def spread_probs(i, o):
                dve.wait_ge(probT_done, group(i, o) + 1)
                for h in range(H):
                    rows = slice(h * S, (h + 1) * S)
                    src = ps_probT[0:S, :].rearrange("p (t r) -> p t r", t=T)[:, :, rows]
                    dve.tensor_copy(probT[rows, :, rows], src).then_inc(probT_ready, 1)

            def add_residual(i, o, t):
                s, g = o % 2, group(i, o)
                dve.wait_ge(out_done, T * g + t + 1)
                if t == 0:
                    dve.wait_ge(x_res_ready, g + 1)
                    dve.wait_ge(norm_ready, 2 * g + 2)
                    if o >= 2:
                        dve.wait_ge(out_stored[s], 16 * (i + o // 2))
                dve.scalar_tensor_tensor(out=y[:, s, t, :], in0=out_bank(t)[:, 0:D],
                                         scalar=inv_sum[:, s, t:t + 1], in1=x_res[:, s, t, :],
                                         op0=ALU.mult, op1=ALU.add).then_inc(y_ready, 1)

            def tile_stats(i, o, t):
                g = group(i, o)
                dve.wait_ge(y_ready, T * g + t + 1)
                if t == 0 and o >= 1:
                    dve.wait_ge(mv_ready, T * g)
                dve.bn_stats(stats[:, t, :], y[:, o % 2, t, :]).then_inc(stats_ready, 1)

            def mean_variance(i, o):
                s, g = o % 2, group(i, o)
                dve.wait_ge(stats_ready, T * g + T)
                if o >= 1:
                    dve.wait_ge(ln_step, 3 * g)
                dve.sem_inc(dve_held, 1)
                for t in range(T):
                    dve.bn_aggr(mean_var[:, s, t, :], stats[:, t, :]).then_inc(mv_ready, 1)
                dve.wait_ge(mv_ready, T * (g + 1))
                dve.tensor_scalar(var_eps[:, :], mean_var[:, s, :, 1], EPS, None,
                                  ALU.add).then_inc(var_ready, 1)

            def h_low(i, o):
                g = group(i, o)
                for c in range(K):
                    dve.wait_ge(h_hi_ready, K * g + c + 1)
                    dve.scalar_tensor_tensor(out=h_lo[:, c, :], in0=wide[c][:, :], scalar=0.0,
                                             in1=h_hi[:, c, :], op0=ALU.max,
                                             op1=ALU.subtract).then_inc(h_lo_ready, 1)

            def step(i, o):
                g = group(i, o)
                more, before = o < GROUPS - 1, o >= 1
                for t in range(T):
                    dve.wait_ge(xw_done, T * g + t + 1)
                    dve.tensor_tensor(xw[:, t, 0:D + 1], xw_bank(t)[:, 0:D + 1], xw_bias[:, :],
                                      ALU.add).then_inc(xw_ready, 1)
                dve.wait_ge(xw_ready, T * (g + 1))
                softmax_scores(i, o)
                for t in range(T):
                    if more:
                        x_low(i, o + 1, t)
                    if before and t >= 1:
                        add_residual(i, o - 1, t - 1)
                softmax_sums(i, o)
                if before:
                    tile_stats(i, o - 1, 0)
                    tile_stats(i, o - 1, 1)
                spread_probs(i, o)
                if before:
                    tile_stats(i, o - 1, 2)
                    add_residual(i, o - 1, 3)
                    tile_stats(i, o - 1, 3)
                    mean_variance(i, o - 1)
                h_low(i, o)

            for t in range(T):
                x_low(0, 0, t)
            steps(dve, step)
            last = GROUPS - 1
            for t in range(T):
                add_residual(0, last, t)
                if t:
                    tile_stats(0, last, t - 1)
            tile_stats(0, last, T - 1)
            mean_variance(0, last)

        @block.tensor
        def _(pe):
            pe.wait_ge(const_ready, 3)
            for c in range(K):
                for n, (loaded, src, banks) in enumerate(((w1_loaded, w1_d, wide), (w2_loaded, w2_d, turn))):
                    if c == 0:
                        pe.wait_ge(loaded, 16)
                    for k in range(K):
                        mm = pe.transpose(banks[c][:, k * P:(k + 1) * P], src[:, k, c * P:(c + 1) * P],
                                          ident[:, :])
                    mm.then_inc(turned_w, 1)
            pe.wait_ge(dep_loaded, 80)
            for n, w in enumerate((w1_dep, w2_dep)):
                for c in range(K):
                    mm = pe.matmul(ps_probT[:, n * K + c:n * K + c + 1], w[:, c * P:(c + 1) * P],
                                   emb1[:, :], start=True, stop=True)
            mm.then_inc(dep_done, 1)
            pe.wait_ge(w_e_act, K)
            pe.wait_ge(w_e_dve, K)
            for k in range(K):
                for c in range(K):
                    mm = pe.matmul(turn[k][:, 0:D], w1_e[:, c, k * P:(k + 1) * P], w2_e[:, c, :],
                                   start=(c == 0), stop=(c == K - 1))
                mm.then_inc(g_done, 1)
            pe.wait_ge(bp_ready, 3)
            for col, (w, v) in enumerate(((w2_e, b1p), (w1_e, b2p))):
                for k in range(K):
                    for c in range(K):
                        pe.matmul(ps_score[:, col * K + k:col * K + k + 1], w[:, c, k * P:(k + 1) * P],
                                  v[:, c:c + 1], start=(c == 0), stop=(c == K - 1))
            for c in range(K):
                mm = pe.matmul(ps_score[:, 2 * K:2 * K + 1], ones[:, :], b1b2[:, c:c + 1],
                               start=(c == 0), stop=(c == K - 1))
            mm.then_inc(uw_done, 1)
            pe.wait_ge(squared, 1)
            pe.matmul(ps_probT[0:1, 2 * K:2 * K + 1], flag_part[:, :], ones[:, 0:1],
                      start=True, stop=True).then_inc(flag_sum, 1)

            pe.wait_ge(flag_ready, 1)
            other_types = pe.value_load(flag[0:1, 0:1], min_val=0, max_val=1)
            with pe.If(other_types > 0):
                pe.wait_ge(ge_load, 16)
                pe.wait_ge(g_lo_ready, K)
                for n, w in enumerate((w1_dep, w2_dep)):
                    for c in range(K):
                        mm = pe.matmul(wide[n][:, c * NT:(c + 1) * NT], w[:, c * P:(c + 1) * P],
                                       embT[:, :], start=True, stop=True)
                mm.then_inc(ge_pe, 1)
                pe.wait_ge(ge_dve, 6)
                pe.wait_ge(weights_ready, 3)
                for n, (w, d) in enumerate(((w1_e, d2T), (w2_e, d1T))):
                    for k in range(K):
                        for c in range(K):
                            pe.matmul(ps_score[:, (2 * k + n) * NT:(2 * k + n + 1) * NT],
                                      w[:, c, k * P:(k + 1) * P], d[:, c, :],
                                      start=(c == 0), stop=(c == K - 1))
                for c in range(K):
                    pe.matmul(ps_probT[0:1, 0:NT], b1p[:, c:c + 1], d2T[:, c, :],
                              start=(c == 0), stop=(c == K - 1))
                for c in range(K):
                    mm = pe.matmul(ps_probT[0:1, NT:2 * NT], ones[:, 0:1], dd[:, c, :],
                                   start=(c == 0), stop=(c == K - 1))
                mm.then_inc(ge_pe, 1)
                pe.wait_ge(ge_act, 2)
                with pe.Fori(0, TILES) as k:
                    n = pe.snap(k)
                    pe.wait_ge(gt_x, n * 16 + 16)
                    for c in range(K):
                        mm = pe.transpose(wide[0][:, c * P:(c + 1) * P], xg[:, c * P:(c + 1) * P], ident[:, :])
                    mm.then_inc(gt_pe, 1)
                    pe.wait_ge(gt_act, n * 2 + 1)
                    for c in range(K):
                        pe.matmul(wide[1][:, 0:2 * NT], xgT[:, c, :], uv[:, c, :], start=(c == 0), stop=False)
                    pe.matmul(wide[1][:, 0:2 * NT], ones[0:1, :], pq_row[:, :], start=False,
                              stop=True).then_inc(gt_pe, 1)
                pe.wait_ge(gt_act, 2 * TILES)

            def turn_x(i, o):
                g, s = group(i, o), o % 2
                pe.wait_ge(x_loaded[s], 16 * (i + o // 2 + 1))
                for t in range(T):
                    if o >= 1 and t < 2:
                        pe.wait_ge(xw_ready, T * (g - 1) + t + 2)
                    elif o >= 1 and t == 2:
                        pe.wait_ge(xw_ready, T * g)
                    elif t == 3:
                        pe.wait_ge(xT_hi_ready, T * g + 1)
                    for c in range(K):
                        mm = pe.transpose(xT_bank(t)[:, c * P:(c + 1) * P], x_in[:, s, t, c * P:(c + 1) * P],
                                          ident[:, :])
                    mm.then_inc(xT_done, 1)

            def three_passes(dst, terms):
                n = K * 3
                at = 0
                for k in range(K):
                    for lhs, rhs in terms(k):
                        mm = pe.matmul(dst, lhs, rhs, start=(at == 0), stop=(at == n - 1))
                        at += 1
                return mm

            def y_product(i, o):
                g = group(i, o)
                pe.wait_ge(xT_lo_ready, T * (g + 1))
                for c in range(K):
                    if o >= 1:
                        pe.wait_ge(h_lo_ready, K * (g - 1) + c + 1)
                    cols = slice(c * P, (c + 1) * P)
                    three_passes(wide[c][:, :], lambda k: (
                        (g_hi[:, k, cols], xT_hi[:, k, :]), (g_hi[:, k, cols], xT_lo[:, k, :]),
                        (g_lo[:, k, cols], xT_hi[:, k, :]))).then_inc(y_done, 1)

            def xw_product(i, o):
                g = group(i, o)
                for t in range(T):
                    if o >= 2 and t < 3:
                        pe.wait_ge(y_ready, T * (g - 2) + t + 2)
                    elif t < 3:
                        pe.wait_ge(xT_hi_ready, T * (g + 1))
                    else:
                        pe.wait_ge(xw_ready, T * g + 1)
                    rows = slice(t * P, (t + 1) * P)
                    three_passes(xw_bank(t)[:, 0:XC], lambda k: (
                        (xT_hi[:, k, rows], gw_hi[:, k, :]), (xT_hi[:, k, rows], gw_lo[:, k, :]),
                        (xT_lo[:, k, rows], gw_hi[:, k, :]))).then_inc(xw_done, 1)

            def scores(i, o):
                g = group(i, o)
                pe.wait_ge(yT_ready, K * (g + 1))
                if o >= 1:
                    pe.wait_ge(soft, SOFT * (g - 1) + H)
                for t in range(T):
                    rows = slice(t * P, (t + 1) * P)
                    for k in range(K):
                        mm = pe.matmul(ps_score[:, rows], yT[:, k, rows], xT[:, k, rows],
                                       start=(k == 0), stop=(k == K - 1))
                mm.then_inc(score_done, 1)

            def out_product(i, o, tiles):
                g = group(i, o)
                if 0 in tiles:
                    pe.wait_ge(h_lo_ready, K * (g + 1))
                for t in tiles:
                    if t < 3 and o < GROUPS - 2:
                        pe.wait_ge(xT_hi_ready, T * (g + 2) + t + 2)
                    elif t < 3 and o == GROUPS - 2:
                        pe.wait_ge(xw_ready, T * (g + 2))
                    elif t < 3:
                        pe.wait_ge(y_ready, T * g)
                    else:
                        pe.wait_ge(y_ready, T * g + 1)
                    rows = slice(t * P, (t + 1) * P)
                    three_passes(out_bank(t)[:, 0:D], lambda k: (
                        (h_hi[:, k, rows], wo_hi[:, k, :]), (h_hi[:, k, rows], wo_lo[:, k, :]),
                        (h_lo[:, k, rows], wo_hi[:, k, :]))).then_inc(out_done, 1)

            def turn_probs(i, o):
                g = group(i, o)
                pe.wait_ge(prob_ready, g + 1)
                if o >= 1:
                    pe.wait_ge(probT_ready, H * g)
                pe.sem_inc(pe_held, 1)
                for t in range(T):
                    mm = pe.transpose(ps_probT[0:S, t * P:(t + 1) * P], prob[:, t, :], ident[:, :])
                mm.then_inc(probT_done, 1)

            def aggregate(i, o):
                g = group(i, o)
                pe.wait_ge(probT_ready, H * (g + 1))
                pe.wait_ge(xw_ready, T * (g + 1))
                for c in range(K):
                    for t in range(T):
                        mm = pe.matmul(wide[c][:, t * P:(t + 1) * P], xw[:, t, c * P:(c + 1) * P],
                                       probT[:, t, :], start=True, stop=True)
                    mm.then_inc(agg_done, 1)

            def step(i, o):
                before, more = o >= 1, o < GROUPS - 1
                y_product(i, o)
                xw_product(i, o)
                scores(i, o)
                if more:
                    turn_x(i, o + 1)
                if before:
                    out_product(i, o - 1, range(0, 3))
                turn_probs(i, o)
                if before:
                    out_product(i, o - 1, range(3, 4))
                aggregate(i, o)

            pe.wait_ge(g_lo_ready, K)
            turn_x(0, 0)
            pe.wait_ge(zeroed, 3)
            pe.wait_ge(weights_ready, 4)
            steps(pe, step)
            out_product(0, GROUPS - 1, range(0, 4))


INPUTS = ("x", "adj", "L0_gnn_dep_emb_table", "L0_gnn_W1_w", "L0_gnn_W1_b", "L0_gnn_W2_w", "L0_gnn_W2_b",
          "L0_gnn_gcn_w", "L0_gnn_gcn_b", "L0_gnn_Wo_w", "L0_gnn_Wo_b")


def kernel(**inputs):
    import concourse.bacc as bacc
    from concourse.bass_utils import run_bass_kernel_spmd

    nc = bacc.Bacc("TRN2", target_bir_lowering=False, num_devices=1)
    arrays, args = {}, []
    for name in INPUTS:
        a = np.ascontiguousarray(inputs[name])
        arrays[f"in_{name}"] = a
        args.append(nc.dram_tensor(f"in_{name}", a.shape, mybir.dt.from_np(a.dtype), kind="ExternalInput").ap())
    shape = arrays["in_x"].shape
    args.append(nc.dram_tensor("out_0", shape, F32, kind="ExternalOutput").ap())
    build(nc, *args)
    r = run_bass_kernel_spmd(nc, [arrays], core_ids=[0])
    return r.results[0]["out_0"]
```

```python
from contextlib import ExitStack

import numpy as np

import concourse.bass as bass
from concourse import mybir

F32 = mybir.dt.float32
F32R = mybir.dt.float32r
I32 = mybir.dt.int32
ALU = mybir.AluOpType
ACT = mybir.ActivationFunctionType
AX = mybir.AxisListType
ds = bass.ds

P = 128
NEG = -1.0e9
EPS = 1.0e-5


def build(nc, x, adj, emb, w1, b1, w2, b2, gcn_w, gcn_b, wo, wo_b, out):
    NGRAPH, S, D = x.shape
    NT, DEP = emb.shape
    K = D // P
    R = NGRAPH * S
    TILES = R // P
    H = P // S
    T = 4
    GROUPS = TILES // T
    GW = T * P
    XC = D + 2
    assert H == 2 and GW == 512 and GROUPS % 2 == 0 and S == 64

    x_rows = x.rearrange("b s d -> (b s) d")
    x_groups = x_rows.rearrange("(g t p) d -> g p t d", t=T, p=P)
    B = 32
    Q = P // B
    F = D // Q
    x_blocks = x_rows.rearrange("(g m b) (q f) -> g q b m f", m=GW // B, b=B, q=Q)
    quadrant = lambda q: slice(q * B, (q + 1) * B)
    x_tiles = x_rows.rearrange("(k p) d -> k p d", p=P)
    out_groups = out.rearrange("b s d -> (b s) d").rearrange("(g t p) d -> g p t d", t=T, p=P)
    adj_tiles = adj.rearrange("b s j -> (b s) j").rearrange("(k p) j -> p k j", p=P)
    chunked = lambda m: m.rearrange("(k p) e -> p k e", p=P)
    as_transposed = lambda m: m.rearrange("(p k) e -> p k e", k=K)
    row_on_all = lambda v: v.rearrange("(a n) -> a n", a=1).broadcast_to((P, D))

    q_scratch = nc.dram_tensor("q_scratch", (P, NT), F32, kind="Internal").ap()

    ctx = ExitStack()
    with ctx:
        sb = lambda name, shape, dt=F32: ctx.enter_context(nc.sbuf_tensor(name, shape, dt))
        sem = lambda name: ctx.enter_context(nc.semaphore(name))
        bank = lambda name: ctx.enter_context(nc.psum_tensor(name, [P, 512], F32))

        ident = sb("ident", [P, P])
        ones = sb("ones", [P, P])
        half = sb("half", [P, 1])
        minus_half = sb("minus_half", [P, T])
        minus_one = sb("minus_one", [P, T])
        w1_d = sb("w1_d", [P, K, D])
        w2_d = sb("w2_d", [P, K, D])
        w1_e = sb("w1_e", [P, K, D])
        w2_e = sb("w2_e", [P, K, D])
        w1_dep = sb("w1_dep", [DEP + 1, D])
        w2_dep = sb("w2_dep", [DEP + 1, D])
        emb_sb = sb("emb_sb", [NT, DEP])
        embT = sb("embT", [DEP + 1, NT])
        u_col = sb("u_col", [P, K])
        w_col = sb("w_col", [P, K])
        gcn_raw = sb("gcn_raw", [P, K, D])
        wo_raw = sb("wo_raw", [P, K, D])
        g_hi = sb("g_hi", [P, K, D], F32R)
        g_lo = sb("g_lo", [P, K, D], F32R)
        gw_hi = sb("gw_hi", [P, K, XC], F32R)
        gw_lo = sb("gw_lo", [P, K, XC], F32R)
        wo_hi = sb("wo_hi", [P, K, D], F32R)
        wo_lo = sb("wo_lo", [P, K, D], F32R)
        xw_bias = sb("xw_bias", [P, D + 1])
        wo_bias = sb("wo_bias", [P, D])
        flag_part = sb("flag_part", [P, 1])
        flag = sb("flag", [1, 1], I32)

        adj_sb = sb("adj_sb", [P, TILES, S], I32)
        bias_sb = sb("bias_sb", [P, TILES, S])

        x_in = sb("x_in", [P, GW // B, F])
        x_res = sb("x_res", [P, 2, T, D])
        xT = sb("xT", [P, 2, K, GW])
        xT_hi = sb("xT_hi", [P, K, GW], F32R)
        xT_lo = sb("xT_lo", [P, K, GW], F32R)
        yT = sb("yT", [P, K, GW])
        xw = sb("xw", [P, T, XC])
        offset = sb("offset", [P, T, S])
        score = sb("score", [P, T, S])
        row_max = sb("row_max", [P, T])
        prob = sb("prob", [P, T, S])
        row_sum = sb("row_sum", [P, T])
        inv_sum = sb("inv_sum", [P, 2, T])
        probT = sb("probT", [P, T, P])
        h_hi = sb("h_hi", [P, K, GW], F32R)
        h_lo = sb("h_lo", [P, K, GW], F32R)
        y = sb("y", [P, 2, T, D])
        stats = sb("stats", [P, T, 6])
        mean_var = sb("mean_var", [P, 2, T, 2])
        var_eps = sb("var_eps", [P, T])
        rstd = sb("rstd", [P, 2, T])
        mean_rstd = sb("mean_rstd", [P, T])
        shift = sb("shift", [P, 2, T])

        bp = sb("bp", [P, K, 2])
        d1T = sb("d1T", [P, K, NT])
        d2T = sb("d2T", [P, K, NT])
        d2b = sb("d2b", [P, K, NT])
        dd = sb("dd", [P, K, NT])
        uv = sb("uv", [P, K, 2 * NT])
        pq_row = sb("pq_row", [1, 2 * NT])
        xg = sb("xg", [P, D])
        xgT = sb("xgT", [P, K, P])
        pq = sb("pq", [P, 2 * NT])
        q_all = sb("q_all", [P, S, NT])
        onehot = sb("onehot", [P, S, NT])
        type_iota = sb("type_iota", [P, NT])

        wide = [bank(f"wide{c}") for c in range(K)]
        turn = [bank(f"turn{t}") for t in range(T)]
        ps_score = bank("ps_score")

        w1_loaded, w2_loaded = sem("w1_loaded"), sem("w2_loaded")
        dep_loaded, emb_loaded, gcn_loaded, wo_loaded, adj_loaded, bias_loaded = (
            sem(n + "_loaded") for n in ("dep", "emb", "gcn", "wo", "adj", "bias"))
        x_loaded = sem("x_loaded")
        res_loaded = [sem(f"res_loaded{s}") for s in range(2)]
        out_stored = [sem(f"out_stored{s}") for s in range(2)]
        const_ready = sem("const_ready")
        turned_w = sem("turned_w")
        w_e_act = sem("w_e_act")
        w_e_dve = sem("w_e_dve")
        turned_emb = sem("turned_emb")
        b2_copied = sem("b2_copied")
        embT_ready = sem("embT_ready")
        dep_done = sem("dep_done")
        uwc_ready = sem("uwc_ready")
        g_done = sem("g_done")
        g_hi_ready = sem("g_hi_ready")
        g_lo_ready = sem("g_lo_ready")
        gw_hi_ready = sem("gw_hi_ready")
        gw_ready = sem("gw_ready")
        wo_hi_ready = sem("wo_hi_ready")
        wo_ready = sem("wo_ready")
        zeroed = sem("zeroed")
        squared = sem("squared")
        flag_sum = sem("flag_sum")
        flag_ready = sem("flag_ready")
        bias_ready = sem("bias_ready")
        xT_ready = sem("xT_ready")
        xT_hi_ready = sem("xT_hi_ready")
        xT_lo_ready = sem("xT_lo_ready")
        x_res_ready = sem("x_res_ready")
        y_done = sem("y_done")
        yT_ready = sem("yT_ready")
        xw_done = sem("xw_done")
        xw_ready = sem("xw_ready")
        score_done = sem("score_done")
        soft = sem("soft")
        prob_ready = sem("prob_ready")
        norm_ready = sem("norm_ready")
        probT_ready = sem("probT_ready")
        agg_done = sem("agg_done")
        h_hi_ready = sem("h_hi_ready")
        h_lo_ready = sem("h_lo_ready")
        out_done = sem("out_done")
        y_ready = sem("y_ready")
        stats_ready = sem("stats_ready")
        mv_ready = sem("mv_ready")
        var_ready = sem("var_ready")
        ln_step = sem("ln_step")
        ln_ready = sem("ln_ready")
        last_ready = sem("last_ready")
        SOFT = H + 5
        PB = Q * (S // B)
        dve_held = sem("dve_held")
        ge_pe, ge_act, ge_dve = sem("ge_pe"), sem("ge_act"), sem("ge_dve")
        GT = 10
        gt_x, gt_q, gt_qb, gt_pe, gt_act, gt_dve = (
            sem("gt_" + n) for n in ("x", "q", "qb", "pe", "act", "dve"))

        block = ctx.enter_context(nc.Block())

        def steps(eng, step):
            step(0, 0)
            step(0, 1)
            with eng.Fori(0, (GROUPS - 4) // 2) as i:
                step(i, 2)
                step(i, 3)
            step(0, GROUPS - 2)
            step(0, GROUPS - 1)

        def group(i, o):
            return 2 * i + o

        @block.sync
        def _(sp):
            def load_x(g):
                for q in range(Q):
                    sp.dma_start(x_in[quadrant(q), :, :], x_blocks[g, q]).then_inc(x_loaded, 16)

            sp.dma_start(w1_d[:, :, :], as_transposed(w1[0:D, :])).then_inc(w1_loaded, 16)
            sp.dma_start(emb_sb[:, :], emb).then_inc(emb_loaded, 16)
            for w, b, dst in ((w1, b1, w1_dep), (w2, b2, w2_dep)):
                sp.dma_start(dst[0:DEP, :], w[D:D + DEP, :]).then_inc(dep_loaded, 16)
                sp.dma_start(dst[DEP:DEP + 1, :], b.rearrange("(a n) -> a n", a=1)).then_inc(dep_loaded, 16)
            sp.dma_start(w2_d[:, :, :], as_transposed(w2[0:D, :])).then_inc(w2_loaded, 16)
            load_x(0)
            sp.dma_start(gcn_raw[:, :, :], as_transposed(gcn_w)).then_inc(gcn_loaded, 16)
            sp.dma_start(adj_sb[:, :, :], adj_tiles).then_inc(adj_loaded, 16)
            sp.wait_ge(xT_ready, 1)
            load_x(1)
            sp.dma_start(wo_raw[:, :, :], chunked(wo)).then_inc(wo_loaded, 16)
            for s in range(2):
                sp.dma_start(x_res[:, s, :, :], x_groups[s]).then_inc(res_loaded[s], 16)

            sp.wait_ge(flag_ready, 1)
            other_types = sp.value_load(flag[0:1, 0:1], min_val=0, max_val=1)
            with sp.If(other_types > 0):
                with sp.Fori(0, TILES) as k:
                    src = sp.snap(k)
                    sp.wait_ge(gt_dve, src * GT + 1)
                    sp.dma_start(xg[:, :], x_tiles[src]).then_inc(gt_x, 16)
                    sp.wait_ge(gt_act, src * 2 + 2)
                    sp.dma_start(q_scratch, pq[:, NT:2 * NT]).then_inc(gt_q, 16)
                    sp.wait_ge(gt_q, src * 16 + 16)
                    for h in range(H):
                        rows = q_scratch[h * S:(h + 1) * S, :].rearrange("(a s) t -> a (s t)", a=1)
                        sp.dma_start(q_all[h * S:(h + 1) * S, :, :].rearrange("p s t -> p (s t)"),
                                     rows.broadcast_to((S, S * NT))).then_inc(gt_qb, 16)

            def load(i, o):
                g = sp.snap(group(i, o))
                sp.wait_ge(xT_ready, g)
                load_x(g)

            def load_residual(i, o):
                g = sp.snap(group(i, o))
                sp.wait_ge(y_ready, T * (g - 1))
                sp.dma_start(x_res[:, o % 2, :, :], x_groups[g]).then_inc(res_loaded[o % 2], 16)

            def store(i, o):
                g = sp.snap(group(i, o))
                sp.wait_ge(ln_ready, T * (g + 1))
                sp.dma_start(out_groups[g], y[:, o % 2, :, :]).then_inc(out_stored[o % 2], 16)

            load(0, 2)
            load(0, 3)
            load_residual(0, 2)
            with sp.Fori(0, (GROUPS - 4) // 2) as i:
                for o in (2, 3):
                    load(i, o + 2)
                    store(i, o - 2)
                    load_residual(i, o + 1)
            store(0, GROUPS - 4)
            load_residual(0, GROUPS - 1)
            store(0, GROUPS - 3)
            store(0, GROUPS - 2)
            for t in range(T):
                sp.wait_ge(last_ready, t + 1)
                sp.dma_start(out_groups[GROUPS - 1][:, t, :], y[:, 1, t, :]).then_inc(out_stored[1], 16)
            sp.wait_ge(out_stored[0], 16 * (GROUPS // 2))
            sp.wait_ge(out_stored[1], 16 * (GROUPS // 2 - 1 + T))

        @block.gpsimd
        def _(pool):
            pool.memset(ident[:, :], 0.0).then_inc(const_ready, 1)
            pool.wait_ge(const_ready, 1)
            pool.affine_select(out=ident[:, :], in_=ident[:, :], compare_op=ALU.not_equal, fill=1.0,
                               base=0, pattern=[[-1, P]], channel_multiplier=1).then_inc(const_ready, 1)
            pool.memset(ones[:, :], 1.0).then_inc(const_ready, 1)
            pool.memset(half[:, :], -0.5).then_inc(const_ready, 1)
            pool.memset(minus_half[:, :], -0.5).then_inc(const_ready, 1)
            pool.memset(minus_one[:, :], -1.0).then_inc(const_ready, 1)
            pool.dma_start(wo_bias[:, :], row_on_all(wo_b)).then_inc(bias_loaded, 16)
            pool.dma_start(xw_bias[:, 0:D], row_on_all(gcn_b)).then_inc(bias_loaded, 16)

            pool.iota(type_iota[:, :], pattern=[[1, NT]], base=0, channel_multiplier=0,
                      allow_small_or_imprecise_dtypes=True).then_inc(const_ready, 1)

            pool.wait_ge(bias_loaded, 32)
            pool.wait_ge(const_ready, 7)

            def residual(i, o):
                s = o % 2
                pool.wait_ge(res_loaded[s], 16 * (i + o // 2 + 1))
                pool.tensor_tensor(x_res[:, s, :, :], x_res[:, s, :, :],
                                   wo_bias[:, :].unsqueeze(1).broadcast_to((P, T, D)),
                                   ALU.add).then_inc(x_res_ready, 1)

            def layer_norm(i, o):
                s, g = o % 2, group(i, o)
                pool.wait_ge(var_ready, g + 1)
                if o >= 2:
                    pool.wait_ge(ln_ready, T * (g - 1))
                pool.tensor_tensor(rstd[:, s, :], var_eps[:, :], minus_half[:, :],
                                   ALU.pow).then_inc(ln_step, 1)
                pool.wait_ge(ln_step, 3 * g + 1)
                pool.tensor_tensor(mean_rstd[:, :], mean_var[:, s, :, 0], rstd[:, s, :],
                                   ALU.mult).then_inc(ln_step, 1)
                pool.wait_ge(ln_step, 3 * g + 2)
                pool.tensor_tensor(shift[:, s, :], mean_rstd[:, :], minus_one[:, :],
                                   ALU.mult).then_inc(ln_step, 1)

            def last_scales(o):
                for t in range(T):
                    pool.wait_ge(var_ready, o + t + 1)
                    if t == 0:
                        pool.wait_ge(ln_ready, T * (o - 1))
                    pool.tensor_tensor(rstd[:, o % 2, t:t + 1], var_eps[:, t:t + 1], minus_half[:, t:t + 1],
                                       ALU.pow).then_inc(ln_step, 1)

            residual(0, 0)
            residual(0, 1)
            layer_norm(0, 0)
            residual(0, 2)
            layer_norm(0, 1)
            with pool.Fori(0, (GROUPS - 4) // 2) as i:
                for o in (2, 3):
                    residual(i, o + 1)
                    layer_norm(i, o)
            residual(0, GROUPS - 1)
            layer_norm(0, GROUPS - 2)
            last_scales(GROUPS - 1)

        @block.scalar
        def _(act):
            act.wait_ge(turned_emb, 1)
            act.activation(embT[0:DEP, :], turn[K][0:DEP, P:P + NT], ACT.Copy).then_inc(embT_ready, 1)
            for c in range(K):
                act.wait_ge(turned_w, c + 1)
                act.activation(w1_e[:, c, :], wide[c][:, 0:D], ACT.Copy).then_inc(w_e_act, 1)
            act.wait_ge(turned_w, 2 * K)
            act.activation(w2_e[:, K - 1, :], turn[K - 1][:, 0:D], ACT.Copy).then_inc(w_e_act, 1)

            def g_high(k):
                act.wait_ge(g_done, k + 1)
                act.activation(g_hi[:, k, :], wide[k][:, 0:D], ACT.Copy).then_inc(g_hi_ready, 1)

            def edge_test():
                act.wait_ge(adj_loaded, 16)
                act.wait_ge(const_ready, 4)
                act.activation(bias_sb[:, :, :], adj_sb[:, :, :], ACT.Square, bias=half[:, 0:1],
                               accum_out=flag_part[:, :]).then_inc(squared, 1)

            def general_path():
                act.wait_ge(flag_ready, 1)
                other_types = act.value_load(flag[0:1, 0:1], min_val=0, max_val=1)
                with act.If(other_types > 0):
                    act.wait_ge(ge_pe, 2)
                    act.activation(uv[:, :, :], ps_score[:, 0:2 * NT * K].rearrange("p (k t) -> p k t", k=K),
                                   ACT.Copy).then_inc(ge_act, 1)
                    act.activation(pq_row[:, :], turn[K][0:1, 0:2 * NT], ACT.Copy).then_inc(ge_act, 1)
                    with act.Fori(0, TILES) as k:
                        n = act.snap(k)
                        act.wait_ge(gt_pe, n * 2 + 1)
                        act.activation(xgT[:, :, :], wide[0][:, 0:D].rearrange("p (k r) -> p k r", k=K),
                                       ACT.Copy).then_inc(gt_act, 1)
                        act.wait_ge(gt_pe, n * 2 + 2)
                        act.activation(pq[:, :], wide[1][:, 0:2 * NT], ACT.Copy).then_inc(gt_act, 1)
                    act.wait_ge(gt_act, 2 * TILES)

            def x_high(i, o):
                g = group(i, o)
                act.wait_ge(xT_ready, g + 1)
                if o >= 1:
                    act.wait_ge(xw_done, T * g)
                for k in range(K):
                    act.activation(xT_hi[:, k, :], xT[:, o % 2, k, :], ACT.Copy).then_inc(xT_hi_ready, 1)

            def result(i, o):
                s, g = o % 2, group(i, o)
                act.wait_ge(ln_step, 3 * g + 3)
                for t in range(T):
                    act.activation(y[:, s, t, :], y[:, s, t, :], ACT.Identity, bias=shift[:, s, t:t + 1],
                                   scale=rstd[:, s, t:t + 1]).then_inc(ln_ready, 1)

            def y_copy(i, o, c):
                act.wait_ge(y_done, K * group(i, o) + c + 1)
                act.activation(yT[:, c, :], wide[c][:, :], ACT.Identity,
                               bias=u_col[:, c:c + 1]).then_inc(yT_ready, 1)

            def exp_scores(i, o):
                act.wait_ge(soft, SOFT * (group(i, o) + 1))
                act.activation(prob[:, :, :], score[:, :, :], ACT.Exp).then_inc(prob_ready, 1)

            def h_high(i, o):
                for c in range(K):
                    act.wait_ge(agg_done, K * group(i, o) + c + 1)
                    act.activation(h_hi[:, c, :], wide[c][:, :], ACT.Relu).then_inc(h_hi_ready, 1)

            def first_step():
                act.wait_ge(uwc_ready, K)
                for c in range(K):
                    y_copy(0, 0, c)
                act.wait_ge(wo_loaded, 16)
                act.activation(wo_hi[:, :, :], wo_raw[:, :, :], ACT.Copy).then_inc(wo_hi_ready, 1)
                general_path()
                x_high(0, 1)
                exp_scores(0, 0)
                for c in range(K):
                    y_copy(0, 1, c)
                h_high(0, 0)

            def step(i, o):
                if o == 0:
                    first_step()
                    return
                if o >= 2:
                    for c in range(K):
                        y_copy(i, o, c)
                    result(i, o - 2)
                if o < GROUPS - 1:
                    x_high(i, o + 1)
                exp_scores(i, o)
                h_high(i, o)

            x_high(0, 0)
            for k in range(K):
                g_high(k)
            act.wait_ge(zeroed, 4)
            act.wait_ge(uwc_ready, 2 * K)
            act.activation(gw_hi[:, :, D], w_col[:, :], ACT.Copy).then_inc(gw_hi_ready, 1)
            act.wait_ge(gcn_loaded, 16)
            act.activation(gw_hi[:, :, 0:D], gcn_raw[:, :, :], ACT.Copy).then_inc(gw_hi_ready, 1)
            edge_test()
            steps(act, step)
            result(0, GROUPS - 2)

        @block.vector
        def _(dve):
            def g_low(k):
                dve.wait_ge(g_hi_ready, k + 1)
                dve.tensor_tensor(g_lo[:, k, :], wide[k][:, 0:D], g_hi[:, k, :],
                                  ALU.subtract).then_inc(g_lo_ready, 1)

            def gw_low():
                dve.wait_ge(zeroed, 4)
                dve.wait_ge(uwc_ready, 2 * K + 1)
                dve.wait_ge(gw_hi_ready, 1)
                dve.tensor_tensor(gw_lo[:, :, D], w_col[:, :], gw_hi[:, :, D],
                                  ALU.subtract).then_inc(gw_ready, 1)
                dve.wait_ge(gw_hi_ready, 2)
                dve.tensor_tensor(gw_lo[:, :, 0:D], gcn_raw[:, :, :], gw_hi[:, :, 0:D],
                                  ALU.subtract).then_inc(gw_ready, 1)
                dve.wait_ge(gw_ready, 2)
                dve.wait_ge(bias_loaded, 32)

            def edge_bias():
                dve.wait_ge(squared, 1)
                dve.tensor_scalar(bias_sb[:, :, :], adj_sb[:, :, :], 0.0, NEG, ALU.is_equal,
                                  ALU.mult).then_inc(bias_ready, 1)
                dve.wait_ge(flag_sum, 1)
                dve.tensor_scalar(flag[:, :], ps_score[0:1, 0:1], R * S / 4.0 + 1.0, None,
                                  ALU.is_gt).then_inc(flag_ready, 1)
                dve.wait_ge(bias_ready, 1)

            def wo_low():
                dve.wait_ge(wo_hi_ready, 1)
                dve.tensor_tensor(wo_lo[:, :, :], wo_raw[:, :, :], wo_hi[:, :, :],
                                  ALU.subtract).then_inc(wo_ready, 1)

            def general_path():
                kind, wrapped, extra = score[:, 0, :], score[:, 1, :], score[:, 2, :]
                dve.wait_ge(flag_ready, 1)
                other_types = dve.value_load(flag[0:1, 0:1], min_val=0, max_val=1)
                with dve.If(other_types > 0):
                    dve.wait_ge(ge_pe, 1)
                    for n, d in ((0, d1T), (1, d2T)):
                        e = wide[n][:, 0:K * NT].rearrange("p (k t) -> p k t", k=K)
                        dve.tensor_copy(bp[:, :, n:n + 1], e[:, :, 1:2]).then_inc(ge_dve, 1)
                        dve.wait_ge(ge_dve, 2 * n + 1)
                        dve.tensor_tensor(d[:, :, :], e, bp[:, :, n:n + 1].broadcast_to((P, K, NT)),
                                          ALU.subtract).then_inc(ge_dve, 1)
                    dve.wait_ge(ge_dve, 4)
                    dve.tensor_tensor(d2b[:, :, :], d2T[:, :, :],
                                      bp[:, :, 1:2].broadcast_to((P, K, NT)),
                                      ALU.add).then_inc(ge_dve, 1)
                    dve.wait_ge(ge_dve, 5)
                    dve.tensor_tensor(dd[:, :, :], d1T[:, :, :], d2b[:, :, :], ALU.mult).then_inc(ge_dve, 1)
                    dve.wait_ge(ge_dve, 6)
                    dve.wait_ge(const_ready, 7)
                    dve.sem_inc(gt_dve, 1)
                    with dve.Fori(0, TILES) as k:
                        n = dve.snap(k)
                        types = adj_sb[:, ds(n, 1), :].squeeze(1)
                        bias = bias_sb[:, ds(n, 1), :].squeeze(1)
                        wide_kind = kind.unsqueeze(2).broadcast_to((P, S, NT))
                        wide_type = type_iota[:, :].unsqueeze(1).broadcast_to((P, S, NT))
                        wide_p = pq[:, 0:NT].unsqueeze(1).broadcast_to((P, S, NT))
                        dve.tensor_scalar(wrapped, types, 0.0, float(NT), ALU.is_lt,
                                          ALU.mult).then_inc(gt_dve, 1)
                        dve.wait_ge(gt_dve, n * GT + 2)
                        dve.tensor_tensor(kind, wrapped, types, ALU.add).then_inc(gt_dve, 1)
                        dve.wait_ge(gt_dve, n * GT + 3)
                        dve.tensor_scalar(kind, kind, 0.0, float(NT - 1), ALU.max,
                                          ALU.min).then_inc(gt_dve, 1)
                        dve.wait_ge(gt_dve, n * GT + 4)
                        dve.tensor_tensor(onehot[:, :, :], wide_kind, wide_type, ALU.is_equal).then_inc(gt_dve, 1)
                        dve.wait_ge(gt_dve, n * GT + 5)
                        dve.wait_ge(gt_qb, n * 16 * H + 16 * H)
                        dve.tensor_tensor(q_all[:, :, :], q_all[:, :, :], wide_p, ALU.add).then_inc(gt_dve, 1)
                        dve.wait_ge(gt_dve, n * GT + 6)
                        dve.tensor_tensor(onehot[:, :, :], onehot[:, :, :], q_all[:, :, :],
                                          ALU.mult).then_inc(gt_dve, 1)
                        dve.wait_ge(gt_dve, n * GT + 7)
                        dve.tensor_reduce(extra, onehot[:, :, :], AX.X, ALU.add).then_inc(gt_dve, 1)
                        dve.tensor_scalar(wrapped, types, 0.0, None, ALU.not_equal).then_inc(gt_dve, 1)
                        dve.wait_ge(gt_dve, n * GT + 9)
                        dve.tensor_tensor(extra, extra, wrapped, ALU.mult).then_inc(gt_dve, 1)
                        dve.wait_ge(gt_dve, n * GT + 10)
                        dve.tensor_tensor(bias, bias, extra, ALU.add).then_inc(gt_dve, 1)
                        dve.wait_ge(gt_dve, n * GT + 11)

            def turn_x(i, o):
                g, s = group(i, o), o % 2
                dve.wait_ge(x_loaded, 16 * Q * (g + 1))
                if o >= 2:
                    dve.wait_ge(score_done, g - 1)
                dve.transpose(xT[:, s, :, :].rearrange("p k (m b) -> p m k b", b=B),
                              x_in[:, :, :].rearrange("p m (a k) -> p m k a", k=K)).then_inc(xT_ready, 1)

            def x_low(i, o, k):
                dve.wait_ge(xT_hi_ready, K * group(i, o) + k + 1)
                dve.tensor_tensor(xT_lo[:, k, :], xT[:, o % 2, k, :], xT_hi[:, k, :],
                                  ALU.subtract).then_inc(xT_lo_ready, 1)

            def turn_probs(i, o):
                g = group(i, o)
                dve.wait_ge(prob_ready, g + 1)
                if o >= 1:
                    dve.wait_ge(agg_done, K * g)
                else:
                    dve.wait_ge(zeroed, 4)
                for q in range(Q):
                    for n in range(S // B):
                        first = q * B // S * S + n * B
                        dve.transpose(probT[first:first + B, :, quadrant(q)],
                                      prob[quadrant(q), :, n * B:(n + 1) * B]).then_inc(probT_ready, 1)

            def score_offsets(i, o):
                g = group(i, o)
                dve.wait_ge(xw_ready, T * (g + 1))
                if o >= 1:
                    dve.wait_ge(soft, SOFT * g)
                dve.scalar_tensor_tensor(out=offset[:, :, :], in0=adj_sb[:, ds(T * g, T), :], scalar=0.0,
                                         in1=xw[:, :, D:D + 1].broadcast_to((P, T, S)),
                                         op0=ALU.not_equal, op1=ALU.mult).then_inc(soft, 1)
                dve.wait_ge(soft, SOFT * g + 1)
                dve.tensor_tensor(offset[:, :, :], offset[:, :, :], bias_sb[:, ds(T * g, T), :],
                                  ALU.add).then_inc(soft, 1)

            def softmax_scores(i, o):
                g = group(i, o)
                dve.wait_ge(score_done, g + 1)
                if o >= 1:
                    dve.wait_ge(prob_ready, g)
                for h in range(H):
                    rows = slice(h * S, (h + 1) * S)
                    src = ps_score[rows, :].rearrange("p (t r) -> p t r", t=T)[:, :, rows]
                    dve.scalar_tensor_tensor(out=score[rows, :, :], in0=adj_sb[rows, ds(T * g, T), :],
                                             scalar=0.0, in1=src, op0=ALU.not_equal,
                                             op1=ALU.mult).then_inc(soft, 1)
                dve.wait_ge(soft, SOFT * g + H + 2)
                dve.tensor_tensor(score[:, :, :], score[:, :, :], offset[:, :, :],
                                  ALU.add).then_inc(soft, 1)
                dve.wait_ge(soft, SOFT * g + H + 3)
                dve.tensor_reduce(row_max[:, :], score[:, :, :], AX.X, ALU.max).then_inc(soft, 1)
                dve.wait_ge(soft, SOFT * g + H + 4)
                dve.tensor_tensor(score[:, :, :], score[:, :, :],
                                  row_max[:, :].unsqueeze(2).broadcast_to((P, T, S)),
                                  ALU.subtract).then_inc(soft, 1)

            def softmax_sums(i, o):
                g = group(i, o)
                dve.wait_ge(prob_ready, g + 1)
                dve.tensor_reduce(row_sum[:, :], prob[:, :, :], AX.X, ALU.add).then_inc(norm_ready, 1)
                dve.wait_ge(norm_ready, 2 * g + 1)
                dve.reciprocal(inv_sum[:, o % 2, :], row_sum[:, :]).then_inc(norm_ready, 1)

            def add_residual(i, o, t):
                s, g = o % 2, group(i, o)
                dve.wait_ge(out_done, T * g + t + 1)
                if t == 0:
                    dve.wait_ge(x_res_ready, g + 1)
                    dve.wait_ge(norm_ready, 2 * g + 2)
                    if o >= 1:
                        dve.wait_ge(out_stored[s], 16 * (i + o // 2))
                dve.scalar_tensor_tensor(out=y[:, s, t, :], in0=turn[t][:, 0:D],
                                         scalar=inv_sum[:, s, t:t + 1], in1=x_res[:, s, t, :],
                                         op0=ALU.mult, op1=ALU.add).then_inc(y_ready, 1)

            def tile_stats(i, o, t):
                g = group(i, o)
                dve.wait_ge(y_ready, T * g + t + 1)
                if t == 0 and o >= 1:
                    dve.wait_ge(mv_ready, T * g)
                dve.bn_stats(stats[:, t, :], y[:, o % 2, t, :]).then_inc(stats_ready, 1)

            def mean_variance(i, o):
                s, g = o % 2, group(i, o)
                dve.wait_ge(stats_ready, T * g + T)
                if o >= 1:
                    dve.wait_ge(ln_step, 3 * g)
                dve.sem_inc(dve_held, 1)
                for t in range(T):
                    dve.bn_aggr(mean_var[:, s, t, :], stats[:, t, :]).then_inc(mv_ready, 1)
                dve.wait_ge(mv_ready, T * g + T)
                dve.tensor_scalar(var_eps[:, :], mean_var[:, s, :, 1], EPS, None,
                                  ALU.add).then_inc(var_ready, 1)

            def last_group(o):
                s = o % 2

                def aggregate_stats(t):
                    if t == 0:
                        dve.wait_ge(ln_step, 3 * o)
                    dve.wait_ge(stats_ready, T * o + t + 1)
                    dve.bn_aggr(mean_var[:, s, t, :], stats[:, t, :]).then_inc(mv_ready, 1)

                def variance(t):
                    dve.wait_ge(mv_ready, T * o + t + 1)
                    dve.tensor_scalar(var_eps[:, t:t + 1], mean_var[:, s, t, 1:2], EPS, None,
                                      ALU.add).then_inc(var_ready, 1)

                def normalise(t):
                    dve.wait_ge(ln_step, 3 * o + t + 1)
                    dve.tensor_scalar(y[:, s, t, :], y[:, s, t, :], mean_var[:, s, t, 0:1],
                                      rstd[:, s, t:t + 1], ALU.subtract, ALU.mult).then_inc(last_ready, 1)

                for t in range(T + 2):
                    if t < T:
                        add_residual(0, o, t)
                    if 1 <= t <= T:
                        aggregate_stats(t - 1)
                    if t < T:
                        tile_stats(0, o, t)
                    if 1 <= t <= T:
                        variance(t - 1)
                    if t >= 2:
                        normalise(t - 2)

            def h_low(i, o):
                g = group(i, o)
                for c in range(K):
                    dve.wait_ge(h_hi_ready, K * g + c + 1)
                    dve.scalar_tensor_tensor(out=h_lo[:, c, :], in0=wide[c][:, :], scalar=0.0,
                                             in1=h_hi[:, c, :], op0=ALU.max,
                                             op1=ALU.subtract).then_inc(h_lo_ready, 1)

            def step(i, o):
                g = group(i, o)
                more, before = o < GROUPS - 1, o >= 1
                if more:
                    turn_x(i, o + 1)
                for t in range(T):
                    dve.wait_ge(xw_done, T * g + t + 1)
                    dve.tensor_tensor(xw[:, t, 0:D + 1], turn[t][:, 0:D + 1], xw_bias[:, :],
                                      ALU.add).then_inc(xw_ready, 1)
                    if o == 0 and t == 1:
                        edge_bias()
                if o == 0:
                    wo_low()
                    general_path()
                score_offsets(i, o)
                if o == 0:
                    for k in range(K):
                        x_low(i, 1, k)
                softmax_scores(i, o)
                if more and o > 0:
                    x_low(i, o + 1, 0)
                turn_probs(i, o)
                if more and o > 0:
                    x_low(i, o + 1, 1)
                    x_low(i, o + 1, 2)
                if before:
                    for t in range(T):
                        add_residual(i, o - 1, t)
                h_low(i, o)
                softmax_sums(i, o)
                if before:
                    for t in range(T):
                        tile_stats(i, o - 1, t)
                    mean_variance(i, o - 1)

            dve.memset(embT[DEP:DEP + 1, :], 1.0).then_inc(zeroed, 1)
            dve.memset(probT[:, :, :], 0.0).then_inc(zeroed, 1)
            dve.memset(gw_hi[:, :, D:XC].bitcast(F32), 0.0).then_inc(zeroed, 1)
            dve.memset(gw_lo[:, :, D:XC].bitcast(F32), 0.0).then_inc(zeroed, 1)
            for c in range(K - 1):
                dve.wait_ge(turned_w, K + c + 1)
                dve.tensor_copy(w2_e[:, c, :], turn[c][:, 0:D]).then_inc(w_e_dve, 1)
            turn_x(0, 0)
            dve.wait_ge(dep_done, 1)
            b1_all, b2_all = ps_score[:, 0:D], turn[K][:, 0:D]
            for k in range(K):
                dve.tensor_tensor_reduce(y[:, 0, k, :], w2_d[:, k, :], b1_all, 1.0, 0.0, ALU.mult, ALU.add,
                                         u_col[:, k:k + 1]).then_inc(uwc_ready, 1)
            for k in range(K):
                x_low(0, 0, k)
                g_low(k)
            for k in range(K):
                dve.tensor_tensor_reduce(y[:, 1, k, :], w1_d[:, k, :], b2_all, 1.0, 0.0, ALU.mult, ALU.add,
                                         w_col[:, k:k + 1]).then_inc(uwc_ready, 1)
            dve.tensor_copy(y[:, 0, K, :], b2_all).then_inc(b2_copied, 1)
            dve.wait_ge(b2_copied, 1)
            dve.tensor_tensor_reduce(y[:, 1, K, :], y[:, 0, K, :], b1_all, 1.0, 0.0, ALU.mult, ALU.add,
                                     xw_bias[:, D:D + 1]).then_inc(uwc_ready, 1)
            gw_low()
            steps(dve, step)
            last_group(GROUPS - 1)

        @block.tensor
        def _(pe):
            pe.wait_ge(const_ready, 3)
            pe.wait_ge(emb_loaded, 16)
            pe.transpose(turn[K][0:DEP, P:P + NT], emb_sb[:, :], ident[0:NT, 0:NT]).then_inc(turned_emb, 1)
            for loaded, src, banks in ((w1_loaded, w1_d, wide), (w2_loaded, w2_d, turn)):
                pe.wait_ge(loaded, 16)
                for c in range(K):
                    for k in range(K):
                        mm = pe.transpose(banks[c][:, k * P:(k + 1) * P], src[:, k, c * P:(c + 1) * P],
                                          ident[:, :])
                    mm.then_inc(turned_w, 1)
            pe.wait_ge(dep_loaded, 64)
            pe.wait_ge(embT_ready, 1)
            pe.wait_ge(zeroed, 1)
            for dst, w in ((ps_score, w1_dep), (turn[K], w2_dep)):
                mm = pe.matmul(dst[:, 0:D], embT[:, 1:2].broadcast_to((DEP + 1, P)), w[:, :],
                               start=True, stop=True)
            mm.then_inc(dep_done, 1)

            def g_rows(k):
                for c in range(K):
                    mm = pe.matmul(wide[k][:, 0:D], w1_e[:, c, k * P:(k + 1) * P], w2_e[:, c, :],
                                   start=(c == 0), stop=(c == K - 1))
                mm.then_inc(g_done, 1)

            def edge_test():
                pe.wait_ge(squared, 1)
                pe.wait_ge(uwc_ready, 2 * K + 1)
                pe.matmul(ps_score[0:1, 0:1], flag_part[:, :], ones[:, 0:1],
                          start=True, stop=True).then_inc(flag_sum, 1)

            def general_path():
                pe.wait_ge(flag_ready, 1)
                other_types = pe.value_load(flag[0:1, 0:1], min_val=0, max_val=1)
                with pe.If(other_types > 0):
                    pe.wait_ge(yT_ready, K)
                    for n, w in enumerate((w1_dep, w2_dep)):
                        for c in range(K):
                            mm = pe.matmul(wide[n][:, c * NT:(c + 1) * NT], w[:, c * P:(c + 1) * P],
                                           embT[:, :], start=True, stop=True)
                    mm.then_inc(ge_pe, 1)
                    pe.wait_ge(ge_dve, 6)
                    for n, (w, d) in enumerate(((w1_e, d2T), (w2_e, d1T))):
                        for k in range(K):
                            for c in range(K):
                                pe.matmul(ps_score[:, (2 * k + n) * NT:(2 * k + n + 1) * NT],
                                          w[:, c, k * P:(k + 1) * P], d[:, c, :],
                                          start=(c == 0), stop=(c == K - 1))
                    for c in range(K):
                        pe.matmul(turn[K][0:1, 0:NT], bp[:, c, 0:1], d2T[:, c, :],
                                  start=(c == 0), stop=(c == K - 1))
                    for c in range(K):
                        mm = pe.matmul(turn[K][0:1, NT:2 * NT], ones[:, 0:1], dd[:, c, :],
                                       start=(c == 0), stop=(c == K - 1))
                    mm.then_inc(ge_pe, 1)
                    pe.wait_ge(ge_act, 2)
                    with pe.Fori(0, TILES) as k:
                        n = pe.snap(k)
                        pe.wait_ge(gt_x, n * 16 + 16)
                        features = lambda c: xg[:, :].rearrange("r (p k) -> r k p", k=K)[:, c, :]
                        for c in range(K):
                            mm = pe.transpose(wide[0][:, c * P:(c + 1) * P], features(c),
                                              ident[:, :])
                        mm.then_inc(gt_pe, 1)
                        pe.wait_ge(gt_act, n * 2 + 1)
                        for c in range(K):
                            pe.matmul(wide[1][:, 0:2 * NT], xgT[:, c, :], uv[:, c, :],
                                      start=(c == 0), stop=False)
                        pe.matmul(wide[1][:, 0:2 * NT], ones[0:1, :], pq_row[:, :], start=False,
                                  stop=True).then_inc(gt_pe, 1)
                    pe.wait_ge(gt_act, 2 * TILES)

            def three_passes(dst, terms, ready=None):
                for k in range(K):
                    if ready:
                        ready(k)
                    for n, (lhs, rhs) in enumerate(terms(k)):
                        mm = pe.matmul(dst, lhs, rhs, start=(k == 0 and n == 0), stop=(k == K - 1 and n == 2))
                return mm

            def y_product(i, o):
                g = group(i, o)

                def parts_ready(k):
                    pe.wait_ge(xT_lo_ready, K * g + k + 1)
                    if o == 0:
                        pe.wait_ge(g_lo_ready, k + 1)

                for c in range(K):
                    if o == 1:
                        pe.wait_ge(yT_ready, c + 1)
                    elif o >= 2:
                        pe.wait_ge(h_lo_ready, K * (g - 1) + c + 1)
                    cols = slice(c * P, (c + 1) * P)
                    three_passes(wide[c][:, :], lambda k: (
                        (g_hi[:, k, cols], xT_hi[:, k, :]), (g_hi[:, k, cols], xT_lo[:, k, :]),
                        (g_lo[:, k, cols], xT_hi[:, k, :])),
                        parts_ready if c == 0 else None).then_inc(y_done, 1)

            def xw_product(i, o):
                g = group(i, o)
                if o == 0:
                    pe.wait_ge(gw_ready, 2)
                for t in range(T):
                    if o >= 2:
                        pe.wait_ge(y_ready, T * (g - 2) + t + 1)
                    elif o == 1:
                        pe.wait_ge(xw_ready, t + 1)
                    rows = slice(t * P, (t + 1) * P)
                    three_passes(turn[t][:, 0:XC], lambda k: (
                        (xT_hi[:, k, rows], gw_hi[:, k, :]), (xT_hi[:, k, rows], gw_lo[:, k, :]),
                        (xT_lo[:, k, rows], gw_hi[:, k, :]))).then_inc(xw_done, 1)
                    if o == 0 and t == 1:
                        edge_test()

            def scores(i, o):
                g = group(i, o)
                pe.wait_ge(yT_ready, K * (g + 1))
                if o >= 1:
                    pe.wait_ge(soft, SOFT * (g - 1) + H + 2)
                for t in range(T):
                    rows = slice(t * P, (t + 1) * P)
                    for k in range(K):
                        mm = pe.matmul(ps_score[:, rows], yT[:, k, rows], xT[:, o % 2, k, rows],
                                       start=(k == 0), stop=(k == K - 1))
                mm.then_inc(score_done, 1)

            def out_product(i, o):
                g = group(i, o)
                if o == 0:
                    pe.wait_ge(wo_ready, 1)
                for t in range(T):
                    if o < GROUPS - 1:
                        pe.wait_ge(xw_ready, T * (g + 1) + t + 1)
                    else:
                        pe.wait_ge(y_ready, T * g)
                    rows = slice(t * P, (t + 1) * P)
                    three_passes(turn[t][:, 0:D], lambda k: (
                        (h_hi[:, k, rows], wo_hi[:, k, :]), (h_hi[:, k, rows], wo_lo[:, k, :]),
                        (h_lo[:, k, rows], wo_hi[:, k, :])),
                        (lambda k: pe.wait_ge(h_lo_ready, K * g + k + 1)) if t == 0 else None
                    ).then_inc(out_done, 1)

            def aggregate(i, o):
                g = group(i, o)
                pe.wait_ge(probT_ready, PB * (g + 1))
                pe.wait_ge(xw_ready, T * (g + 1))
                if o == 0:
                    pe.wait_ge(zeroed, 4)
                for c in range(K):
                    if o == 0:
                        pe.wait_ge(yT_ready, K + c + 1)
                    for t in range(T):
                        mm = pe.matmul(wide[c][:, t * P:(t + 1) * P], xw[:, t, c * P:(c + 1) * P],
                                       probT[:, t, :], start=True, stop=True)
                    mm.then_inc(agg_done, 1)

            def step(i, o):
                if o != 1:
                    y_product(i, o)
                xw_product(i, o)
                if o == 0:
                    general_path()
                scores(i, o)
                if o >= 1:
                    out_product(i, o - 1)
                else:
                    y_product(i, 1)
                aggregate(i, o)

            pe.wait_ge(w_e_act, K + 1)
            pe.wait_ge(w_e_dve, K - 1)
            for k in range(K):
                g_rows(k)
            steps(pe, step)
            out_product(0, GROUPS - 1)


INPUTS = ("x", "adj", "L0_gnn_dep_emb_table", "L0_gnn_W1_w", "L0_gnn_W1_b", "L0_gnn_W2_w", "L0_gnn_W2_b",
          "L0_gnn_gcn_w", "L0_gnn_gcn_b", "L0_gnn_Wo_w", "L0_gnn_Wo_b")


def kernel(**inputs):
    import concourse.bacc as bacc
    from concourse.bass_utils import run_bass_kernel_spmd

    nc = bacc.Bacc("TRN2", target_bir_lowering=False, num_devices=1)
    arrays, args = {}, []
    for name in INPUTS:
        a = np.ascontiguousarray(inputs[name])
        arrays[f"in_{name}"] = a
        args.append(nc.dram_tensor(f"in_{name}", a.shape, mybir.dt.from_np(a.dtype), kind="ExternalInput").ap())
    shape = arrays["in_x"].shape
    args.append(nc.dram_tensor("out_0", shape, F32, kind="ExternalOutput").ap())
    build(nc, *args)
    r = run_bass_kernel_spmd(nc, [arrays], core_ids=[0])
    return r.results[0]["out_0"]
```

```python
from contextlib import ExitStack

import numpy as np

import concourse.bass as bass
from concourse import mybir

F32 = mybir.dt.float32
F32R = mybir.dt.float32r
I32 = mybir.dt.int32
ALU = mybir.AluOpType
ACT = mybir.ActivationFunctionType
AX = mybir.AxisListType
ds = bass.ds

P = 128
NEG = -1.0e9
WARM = (8, 4, 1)
EPS = 1.0e-5


def build(nc, x, adj, emb, w1, b1, w2, b2, gcn_w, gcn_b, wo, wo_b, out):
    NGRAPH, S, D = x.shape
    NT, DEP = emb.shape
    K = D // P
    R = NGRAPH * S
    TILES = R // P
    H = P // S
    T = 4
    GROUPS = TILES // T
    GW = T * P
    PIECES = 4
    PIECE = TILES // PIECES
    XC = D + 2
    assert H == 2 and GW == 512 and GROUPS % 2 == 0 and S == 64

    x_rows = x.rearrange("b s d -> (b s) d")
    x_groups = x_rows.rearrange("(g t p) d -> g p t d", t=T, p=P)
    B = 32
    Q = P // B
    F = D // Q
    x_blocks = x_rows.rearrange("(g m b) (q f) -> g q b m f", m=GW // B, b=B, q=Q)
    quadrant = lambda q: slice(q * B, (q + 1) * B)
    x_tiles = x_rows.rearrange("(k p) d -> k p d", p=P)
    out_groups = out.rearrange("b s d -> (b s) d").rearrange("(g t p) d -> g p t d", t=T, p=P)
    adj_tiles = adj.rearrange("b s j -> (b s) j").rearrange("(k p) j -> p k j", p=P)
    chunked = lambda m: m.rearrange("(k p) e -> p k e", p=P)
    as_transposed = lambda m: m.rearrange("(p k) e -> p k e", k=K)
    row_on_all = lambda v: v.rearrange("(a n) -> a n", a=1).broadcast_to((P, D))

    q_scratch = nc.dram_tensor("q_scratch", (P, NT), F32, kind="Internal").ap()

    ctx = ExitStack()
    with ctx:
        sb = lambda name, shape, dt=F32: ctx.enter_context(nc.sbuf_tensor(name, shape, dt))
        sem = lambda name: ctx.enter_context(nc.semaphore(name))
        bank = lambda name: ctx.enter_context(nc.psum_tensor(name, [P, 512], F32))

        ident = sb("ident", [P, P])
        ones = sb("ones", [P, P])
        half = sb("half", [P, 1])
        minus_half = sb("minus_half", [P, T])
        minus_one = sb("minus_one", [P, T])
        w1_d = sb("w1_d", [P, K, D])
        w2_d = sb("w2_d", [P, K, D])
        w1_e = sb("w1_e", [P, K, D])
        w2_e = sb("w2_e", [P, K, D])
        w1_dep = sb("w1_dep", [DEP + 1, D])
        w2_dep = sb("w2_dep", [DEP + 1, D])
        emb_sb = sb("emb_sb", [NT, DEP])
        embT = sb("embT", [DEP + 1, NT])
        u_col = sb("u_col", [P, K])
        w_col = sb("w_col", [P, K])
        gcn_raw = sb("gcn_raw", [P, K, D])
        wo_raw = sb("wo_raw", [P, K, D])
        g_hi = sb("g_hi", [P, K, D], F32R)
        g_lo = sb("g_lo", [P, K, D], F32R)
        gw_hi = sb("gw_hi", [P, K, XC], F32R)
        gw_lo = sb("gw_lo", [P, K, XC], F32R)
        wo_hi = sb("wo_hi", [P, K, D], F32R)
        wo_lo = sb("wo_lo", [P, K, D], F32R)
        xw_bias = sb("xw_bias", [P, D + 1])
        wo_bias = sb("wo_bias", [P, D])
        flag_part = sb("flag_part", [P, PIECES])
        flag_parts = sb("flag_parts", [1, 1])
        flag = sb("flag", [1, 1], I32)

        adj_sb = sb("adj_sb", [P, TILES, S], I32)
        bias_sb = sb("bias_sb", [P, TILES, S])

        x_in = sb("x_in", [P, GW // B, F])
        x_res = sb("x_res", [P, 2, T, D])
        xT = sb("xT", [P, 2, K, GW])
        xT_hi = sb("xT_hi", [P, K, GW], F32R)
        xT_lo = sb("xT_lo", [P, K, GW], F32R)
        yT = sb("yT", [P, K, GW])
        xw = sb("xw", [P, T, XC])
        offset = sb("offset", [P, T, S])
        score = sb("score", [P, T, S])
        row_max = sb("row_max", [P, T])
        prob = sb("prob", [P, T, S])
        row_sum = sb("row_sum", [P, T])
        inv_sum = sb("inv_sum", [P, 2, T])
        probT = sb("probT", [P, T, P])
        h_hi = sb("h_hi", [P, K, GW], F32R)
        h_lo = sb("h_lo", [P, K, GW], F32R)
        y = sb("y", [P, 2, T, D])
        stats = sb("stats", [P, T, 6])
        mean_var = sb("mean_var", [P, 2, T, 2])
        var_eps = sb("var_eps", [P, T])
        rstd = sb("rstd", [P, 2, T])
        mean_rstd = sb("mean_rstd", [P, T])
        shift = sb("shift", [P, 2, T])

        bp = sb("bp", [P, K, 2])
        d1T = sb("d1T", [P, K, NT])
        d2T = sb("d2T", [P, K, NT])
        d2b = sb("d2b", [P, K, NT])
        dd = sb("dd", [P, K, NT])
        uv = sb("uv", [P, K, 2 * NT])
        pq_row = sb("pq_row", [1, 2 * NT])
        xg = sb("xg", [P, D])
        xgT = sb("xgT", [P, K, P])
        pq = sb("pq", [P, 2 * NT])
        q_all = sb("q_all", [P, S, NT])
        onehot = sb("onehot", [P, S, NT])
        type_iota = sb("type_iota", [P, NT])

        wide = [bank(f"wide{c}") for c in range(K)]
        turn = [bank(f"turn{t}") for t in range(T)]
        ps_score = bank("ps_score")

        w1_loaded = [sem(f"w1_loaded{k}") for k in range(K)]
        w2_loaded = sem("w2_loaded")
        dep_loaded, emb_loaded, gcn_loaded, wo_loaded, bias_loaded = (
            sem(n + "_loaded") for n in ("dep", "emb", "gcn", "wo", "bias"))
        adj_loaded = [sem(f"adj_loaded{n}") for n in range(PIECES)]
        x_loaded = sem("x_loaded")
        res_loaded = [sem(f"res_loaded{s}") for s in range(2)]
        out_stored = [sem(f"out_stored{s}") for s in range(2)]
        ones_ready = sem("ones_ready")
        const_ready = sem("const_ready")
        turned_w = sem("turned_w")
        w_e_act = sem("w_e_act")
        w_e_dve = sem("w_e_dve")
        turned_emb = sem("turned_emb")
        b2_copied = sem("b2_copied")
        embT_ready = sem("embT_ready")
        dep_done = sem("dep_done")
        uwc_ready = sem("uwc_ready")
        g_done = sem("g_done")
        g_hi_ready = sem("g_hi_ready")
        g_lo_ready = sem("g_lo_ready")
        gw_hi_ready = sem("gw_hi_ready")
        gw_ready = sem("gw_ready")
        wo_hi_ready = sem("wo_hi_ready")
        wo_ready = sem("wo_ready")
        zeroed = sem("zeroed")
        squared = sem("squared")
        flag_sum = sem("flag_sum")
        flag_added = sem("flag_added")
        flag_ready = sem("flag_ready")
        bias_ready = sem("bias_ready")
        xT_ready = sem("xT_ready")
        xT_hi_ready = sem("xT_hi_ready")
        xT_lo_ready = sem("xT_lo_ready")
        x_res_ready = sem("x_res_ready")
        y_done = sem("y_done")
        yT_ready = sem("yT_ready")
        xw_done = sem("xw_done")
        xw_ready = sem("xw_ready")
        score_done = sem("score_done")
        soft = sem("soft")
        prob_ready = sem("prob_ready")
        norm_ready = sem("norm_ready")
        probT_ready = sem("probT_ready")
        agg_done = sem("agg_done")
        h_hi_ready = sem("h_hi_ready")
        h_lo_ready = sem("h_lo_ready")
        out_done = sem("out_done")
        y_ready = sem("y_ready")
        stats_ready = sem("stats_ready")
        mv_ready = sem("mv_ready")
        var_ready = sem("var_ready")
        ln_step = sem("ln_step")
        ln_ready = sem("ln_ready")
        last_ready = sem("last_ready")
        SOFT = H + 5
        PB = Q * (S // B)
        dve_held = sem("dve_held")
        ge_pe, ge_act, ge_dve = sem("ge_pe"), sem("ge_act"), sem("ge_dve")
        GT = 10
        gt_x, gt_q, gt_qb, gt_pe, gt_act, gt_dve = (
            sem("gt_" + n) for n in ("x", "q", "qb", "pe", "act", "dve"))

        block = ctx.enter_context(nc.Block())

        def steps(eng, step):
            step(0, 0)
            step(0, 1)
            with eng.Fori(0, (GROUPS - 4) // 2) as i:
                step(i, 2)
                step(i, 3)
            step(0, GROUPS - 2)
            step(0, GROUPS - 1)

        def group(i, o):
            return 2 * i + o

        @block.sync
        def _(sp):
            def load_x(g):
                for q in range(Q):
                    sp.dma_start(x_in[quadrant(q), :, :], x_blocks[g, q]).then_inc(x_loaded, 16)

            for k in range(K):
                sp.dma_start(w1_d[:, k, :], as_transposed(w1[0:D, :])[:, k, :]).then_inc(w1_loaded[k], 16)
            sp.dma_start(w2_d[:, :, :], as_transposed(w2[0:D, :])).then_inc(w2_loaded, 16)
            sp.dma_start(emb_sb[:, :], emb).then_inc(emb_loaded, 16)
            for w, b, dst in ((w1, b1, w1_dep), (w2, b2, w2_dep)):
                sp.dma_start(dst[0:DEP, :], w[D:D + DEP, :]).then_inc(dep_loaded, 16)
                sp.dma_start(dst[DEP:DEP + 1, :], b.rearrange("(a n) -> a n", a=1)).then_inc(dep_loaded, 16)
            load_x(0)
            sp.dma_start(gcn_raw[:, :, :], as_transposed(gcn_w)).then_inc(gcn_loaded, 16)
            for n in range(PIECES):
                tiles = slice(n * PIECE, (n + 1) * PIECE)
                sp.dma_start(adj_sb[:, tiles, :], adj_tiles[:, tiles, :]).then_inc(adj_loaded[n], 16)
            sp.wait_ge(xT_ready, K)
            load_x(1)
            sp.dma_start(wo_raw[:, :, :], chunked(wo)).then_inc(wo_loaded, 16)
            for s in range(2):
                sp.dma_start(x_res[:, s, :, :], x_groups[s]).then_inc(res_loaded[s], 16)

            sp.wait_ge(flag_ready, 1)
            other_types = sp.value_load(flag[0:1, 0:1], min_val=0, max_val=1)
            with sp.If(other_types > 0):
                with sp.Fori(0, TILES) as k:
                    src = sp.snap(k)
                    sp.wait_ge(gt_dve, src * GT + 1)
                    sp.dma_start(xg[:, :], x_tiles[src]).then_inc(gt_x, 16)
                    sp.wait_ge(gt_act, src * 2 + 2)
                    sp.dma_start(q_scratch, pq[:, NT:2 * NT]).then_inc(gt_q, 16)
                    sp.wait_ge(gt_q, src * 16 + 16)
                    for h in range(H):
                        rows = q_scratch[h * S:(h + 1) * S, :].rearrange("(a s) t -> a (s t)", a=1)
                        sp.dma_start(q_all[h * S:(h + 1) * S, :, :].rearrange("p s t -> p (s t)"),
                                     rows.broadcast_to((S, S * NT))).then_inc(gt_qb, 16)

            def load(i, o):
                g = sp.snap(group(i, o))
                sp.wait_ge(xT_ready, K * g)
                load_x(g)

            def load_residual(i, o):
                g = sp.snap(group(i, o))
                sp.wait_ge(y_ready, T * (g - 1))
                sp.dma_start(x_res[:, o % 2, :, :], x_groups[g]).then_inc(res_loaded[o % 2], 16)

            def store(i, o):
                g = sp.snap(group(i, o))
                sp.wait_ge(ln_ready, T * (g + 1))
                sp.dma_start(out_groups[g], y[:, o % 2, :, :]).then_inc(out_stored[o % 2], 16)

            load(0, 2)
            load(0, 3)
            load_residual(0, 2)
            with sp.Fori(0, (GROUPS - 4) // 2) as i:
                for o in (2, 3):
                    load(i, o + 2)
                    store(i, o - 2)
                    load_residual(i, o + 1)
            store(0, GROUPS - 4)
            load_residual(0, GROUPS - 1)
            store(0, GROUPS - 3)
            for g in (GROUPS - 2, GROUPS - 1):
                for t in range(T):
                    if g == GROUPS - 1 and t == T - 1:
                        sp.wait_ge(last_ready, 1)
                    else:
                        sp.wait_ge(ln_ready, T * g + t + 1)
                    sp.dma_start(out_groups[g][:, t, :], y[:, g % 2, t, :]).then_inc(out_stored[g % 2], 16)
            sp.wait_ge(out_stored[0], 16 * (GROUPS // 2 - 1 + T))
            sp.wait_ge(out_stored[1], 16 * (GROUPS // 2 - 1 + T))

        @block.gpsimd
        def _(pool):
            pool.memset(ident[:, :], 0.0).then_inc(const_ready, 1)
            pool.wait_ge(const_ready, 1)
            pool.affine_select(out=ident[:, :], in_=ident[:, :], compare_op=ALU.not_equal, fill=1.0,
                               base=0, pattern=[[-1, P]], channel_multiplier=1).then_inc(const_ready, 1)
            pool.memset(half[:, :], -0.5).then_inc(const_ready, 1)
            pool.memset(minus_half[:, :], -0.5).then_inc(const_ready, 1)
            pool.memset(minus_one[:, :], -1.0).then_inc(const_ready, 1)
            pool.dma_start(wo_bias[:, :], row_on_all(wo_b)).then_inc(bias_loaded, 16)
            pool.dma_start(xw_bias[:, 0:D], row_on_all(gcn_b)).then_inc(bias_loaded, 16)

            pool.iota(type_iota[:, :], pattern=[[1, NT]], base=0, channel_multiplier=0,
                      allow_small_or_imprecise_dtypes=True).then_inc(const_ready, 1)

            pool.wait_ge(bias_loaded, 32)
            pool.wait_ge(const_ready, 6)

            def residual(i, o):
                s = o % 2
                pool.wait_ge(res_loaded[s], 16 * (i + o // 2 + 1))
                pool.tensor_tensor(x_res[:, s, :, :], x_res[:, s, :, :],
                                   wo_bias[:, :].unsqueeze(1).broadcast_to((P, T, D)),
                                   ALU.add).then_inc(x_res_ready, 1)

            def layer_norm(i, o):
                s, g = o % 2, group(i, o)
                pool.wait_ge(var_ready, g + 1)
                if o >= 2:
                    pool.wait_ge(ln_ready, T * (g - 1))
                pool.tensor_tensor(rstd[:, s, :], var_eps[:, :], minus_half[:, :],
                                   ALU.pow).then_inc(ln_step, 1)
                pool.wait_ge(ln_step, 3 * g + 1)
                pool.tensor_tensor(mean_rstd[:, :], mean_var[:, s, :, 0], rstd[:, s, :],
                                   ALU.mult).then_inc(ln_step, 1)
                pool.wait_ge(ln_step, 3 * g + 2)
                pool.tensor_tensor(shift[:, s, :], mean_rstd[:, :], minus_one[:, :],
                                   ALU.mult).then_inc(ln_step, 1)

            def last_scales(o):
                s = o % 2
                steps_done = 3 * o
                for t in range(T):
                    pool.wait_ge(var_ready, o + t + 1)
                    if t == 0:
                        pool.wait_ge(ln_ready, T * (o - 1))
                    pool.tensor_tensor(rstd[:, s, t:t + 1], var_eps[:, t:t + 1], minus_half[:, t:t + 1],
                                       ALU.pow).then_inc(ln_step, 1)
                    if t < T - 1:
                        pool.wait_ge(ln_step, steps_done + 1)
                        pool.tensor_tensor(mean_rstd[:, t:t + 1], mean_var[:, s, t, 0:1], rstd[:, s, t:t + 1],
                                           ALU.mult).then_inc(ln_step, 1)
                        pool.wait_ge(ln_step, steps_done + 2)
                        pool.tensor_tensor(shift[:, s, t:t + 1], mean_rstd[:, t:t + 1], minus_one[:, t:t + 1],
                                           ALU.mult).then_inc(ln_step, 1)
                    steps_done += 3

            residual(0, 0)
            residual(0, 1)
            layer_norm(0, 0)
            residual(0, 2)
            layer_norm(0, 1)
            with pool.Fori(0, (GROUPS - 4) // 2) as i:
                for o in (2, 3):
                    residual(i, o + 1)
                    layer_norm(i, o)
            residual(0, GROUPS - 1)
            layer_norm(0, GROUPS - 2)
            last_scales(GROUPS - 1)

        @block.scalar
        def _(act):
            for c in range(K):
                act.wait_ge(turned_w, c + 1)
                act.activation(w1_e[:, c, :], wide[c][:, 0:D], ACT.Copy).then_inc(w_e_act, 1)
            act.wait_ge(turned_w, K + 2)
            act.activation(w2_e[:, 1, :], turn[1][:, 0:D], ACT.Copy).then_inc(w_e_act, 1)

            act.wait_ge(turned_emb, 1)
            act.activation(embT[0:DEP, :], turn[K][0:DEP, P:P + NT], ACT.Copy).then_inc(embT_ready, 1)

            def g_high(k):
                act.wait_ge(g_done, k + 1)
                act.activation(g_hi[:, k, :], wide[k][:, 0:D], ACT.Copy).then_inc(g_hi_ready, 1)

            def edge_test(n):
                act.wait_ge(adj_loaded[n], 16)
                tiles = slice(n * PIECE, (n + 1) * PIECE)
                act.activation(bias_sb[:, tiles, :], adj_sb[:, tiles, :], ACT.Square, bias=half[:, 0:1],
                               accum_out=flag_part[:, n:n + 1]).then_inc(squared, 1)

            def general_path():
                act.wait_ge(flag_ready, 1)
                other_types = act.value_load(flag[0:1, 0:1], min_val=0, max_val=1)
                with act.If(other_types > 0):
                    act.wait_ge(ge_pe, 2)
                    act.activation(uv[:, :, :], ps_score[:, 0:2 * NT * K].rearrange("p (k t) -> p k t", k=K),
                                   ACT.Copy).then_inc(ge_act, 1)
                    act.activation(pq_row[:, :], turn[K][0:1, 0:2 * NT], ACT.Copy).then_inc(ge_act, 1)
                    with act.Fori(0, TILES) as k:
                        n = act.snap(k)
                        act.wait_ge(gt_pe, n * 2 + 1)
                        act.activation(xgT[:, :, :], wide[0][:, 0:D].rearrange("p (k r) -> p k r", k=K),
                                       ACT.Copy).then_inc(gt_act, 1)
                        act.wait_ge(gt_pe, n * 2 + 2)
                        act.activation(pq[:, :], wide[1][:, 0:2 * NT], ACT.Copy).then_inc(gt_act, 1)
                    act.wait_ge(gt_act, 2 * TILES)

            def x_high(i, o):
                g = group(i, o)
                if o >= 1:
                    act.wait_ge(xw_done, T * g)
                for k in range(K):
                    act.wait_ge(xT_ready, K * g + k + 1)
                    act.activation(xT_hi[:, k, :], xT[:, o % 2, k, :], ACT.Copy).then_inc(xT_hi_ready, 1)

            def result(i, o):
                s, g = o % 2, group(i, o)
                act.wait_ge(ln_step, 3 * g + 3)
                for t in range(T):
                    act.activation(y[:, s, t, :], y[:, s, t, :], ACT.Identity, bias=shift[:, s, t:t + 1],
                                   scale=rstd[:, s, t:t + 1]).then_inc(ln_ready, 1)

            def last_result(t):
                s = (GROUPS - 1) % 2
                act.wait_ge(ln_step, 3 * (GROUPS - 1 + t + 1))
                act.activation(y[:, s, t, :], y[:, s, t, :], ACT.Identity, bias=shift[:, s, t:t + 1],
                               scale=rstd[:, s, t:t + 1]).then_inc(ln_ready, 1)

            def y_copy(i, o, c):
                act.wait_ge(y_done, K * group(i, o) + c + 1)
                act.activation(yT[:, c, :], wide[c][:, :], ACT.Identity,
                               bias=u_col[:, c:c + 1]).then_inc(yT_ready, 1)

            def exp_scores(i, o):
                act.wait_ge(soft, SOFT * (group(i, o) + 1))
                act.activation(prob[:, :, :], score[:, :, :], ACT.Exp).then_inc(prob_ready, 1)

            def h_high(i, o):
                for c in range(K):
                    act.wait_ge(agg_done, K * group(i, o) + c + 1)
                    act.activation(h_hi[:, c, :], wide[c][:, :], ACT.Relu).then_inc(h_hi_ready, 1)

            def first_step():
                act.wait_ge(uwc_ready, K)
                for c in range(K):
                    y_copy(0, 0, c)
                general_path()
                x_high(0, 1)
                exp_scores(0, 0)
                for c in range(K):
                    y_copy(0, 1, c)
                act.wait_ge(wo_loaded, 16)
                act.activation(wo_hi[:, :, :], wo_raw[:, :, :], ACT.Copy).then_inc(wo_hi_ready, 1)
                h_high(0, 0)

            def step(i, o):
                if o == 0:
                    first_step()
                    return
                if o >= 2:
                    for c in range(K):
                        y_copy(i, o, c)
                    result(i, o - 2)
                if o < GROUPS - 1:
                    x_high(i, o + 1)
                exp_scores(i, o)
                h_high(i, o)

            x_high(0, 0)
            for k in range(K):
                g_high(k)
            act.wait_ge(gcn_loaded, 16)
            act.activation(gw_hi[:, :, 0:D], gcn_raw[:, :, :], ACT.Copy).then_inc(gw_hi_ready, 1)
            act.wait_ge(const_ready, 3)
            edge_test(0)
            edge_test(1)
            act.wait_ge(zeroed, 4)
            act.wait_ge(uwc_ready, 2 * K)
            act.activation(gw_hi[:, :, D], w_col[:, :], ACT.Copy).then_inc(gw_hi_ready, 1)
            edge_test(2)
            edge_test(3)
            steps(act, step)
            result(0, GROUPS - 2)
            for t in range(T - 1):
                last_result(t)

        @block.vector
        def _(dve):
            def g_low(k):
                dve.wait_ge(g_hi_ready, k + 1)
                dve.tensor_tensor(g_lo[:, k, :], wide[k][:, 0:D], g_hi[:, k, :],
                                  ALU.subtract).then_inc(g_lo_ready, 1)

            def gw_low():
                dve.wait_ge(gw_hi_ready, 1)
                dve.tensor_tensor(gw_lo[:, :, 0:D], gcn_raw[:, :, :], gw_hi[:, :, 0:D],
                                  ALU.subtract).then_inc(gw_ready, 1)

            def w_low():
                dve.wait_ge(zeroed, 4)
                dve.wait_ge(uwc_ready, 2 * K + 1)
                dve.wait_ge(gw_hi_ready, 2)
                dve.tensor_tensor(gw_lo[:, :, D], w_col[:, :], gw_hi[:, :, D],
                                  ALU.subtract).then_inc(gw_ready, 1)
                dve.wait_ge(gw_ready, 2)
                dve.wait_ge(bias_loaded, 32)

            def edge_bias(pieces):
                for n in pieces:
                    dve.wait_ge(squared, n + 1)
                    tiles = slice(n * PIECE, (n + 1) * PIECE)
                    dve.tensor_scalar(bias_sb[:, tiles, :], adj_sb[:, tiles, :], 0.0, NEG, ALU.is_equal,
                                      ALU.mult).then_inc(bias_ready, 1)

            bias_pieces = ((0,), (1, 2), (3,), ())

            def edge_flag():
                dve.wait_ge(flag_sum, 1)
                dve.tensor_reduce(flag_parts[:, :], ps_score[0:1, 0:PIECES], AX.X, ALU.add).then_inc(flag_added, 1)
                dve.wait_ge(flag_added, 1)
                dve.tensor_scalar(flag[:, :], flag_parts[:, :], R * S / 4.0 + 1.0, None,
                                  ALU.is_gt).then_inc(flag_ready, 1)

            def wo_low():
                dve.wait_ge(wo_hi_ready, 1)
                dve.tensor_tensor(wo_lo[:, :, :], wo_raw[:, :, :], wo_hi[:, :, :],
                                  ALU.subtract).then_inc(wo_ready, 1)

            def general_path():
                kind, wrapped, extra = score[:, 0, :], score[:, 1, :], score[:, 2, :]
                dve.wait_ge(flag_ready, 1)
                other_types = dve.value_load(flag[0:1, 0:1], min_val=0, max_val=1)
                with dve.If(other_types > 0):
                    dve.wait_ge(ge_pe, 1)
                    for n, d in ((0, d1T), (1, d2T)):
                        e = wide[n][:, 0:K * NT].rearrange("p (k t) -> p k t", k=K)
                        dve.tensor_copy(bp[:, :, n:n + 1], e[:, :, 1:2]).then_inc(ge_dve, 1)
                        dve.wait_ge(ge_dve, 2 * n + 1)
                        dve.tensor_tensor(d[:, :, :], e, bp[:, :, n:n + 1].broadcast_to((P, K, NT)),
                                          ALU.subtract).then_inc(ge_dve, 1)
                    dve.wait_ge(ge_dve, 4)
                    dve.tensor_tensor(d2b[:, :, :], d2T[:, :, :],
                                      bp[:, :, 1:2].broadcast_to((P, K, NT)),
                                      ALU.add).then_inc(ge_dve, 1)
                    dve.wait_ge(ge_dve, 5)
                    dve.tensor_tensor(dd[:, :, :], d1T[:, :, :], d2b[:, :, :], ALU.mult).then_inc(ge_dve, 1)
                    dve.wait_ge(ge_dve, 6)
                    dve.wait_ge(const_ready, 6)
                    dve.sem_inc(gt_dve, 1)
                    with dve.Fori(0, TILES) as k:
                        n = dve.snap(k)
                        types = adj_sb[:, ds(n, 1), :].squeeze(1)
                        bias = bias_sb[:, ds(n, 1), :].squeeze(1)
                        wide_kind = kind.unsqueeze(2).broadcast_to((P, S, NT))
                        wide_type = type_iota[:, :].unsqueeze(1).broadcast_to((P, S, NT))
                        wide_p = pq[:, 0:NT].unsqueeze(1).broadcast_to((P, S, NT))
                        dve.tensor_scalar(wrapped, types, 0.0, float(NT), ALU.is_lt,
                                          ALU.mult).then_inc(gt_dve, 1)
                        dve.wait_ge(gt_dve, n * GT + 2)
                        dve.tensor_tensor(kind, wrapped, types, ALU.add).then_inc(gt_dve, 1)
                        dve.wait_ge(gt_dve, n * GT + 3)
                        dve.tensor_scalar(kind, kind, 0.0, float(NT - 1), ALU.max,
                                          ALU.min).then_inc(gt_dve, 1)
                        dve.wait_ge(gt_dve, n * GT + 4)
                        dve.tensor_tensor(onehot[:, :, :], wide_kind, wide_type, ALU.is_equal).then_inc(gt_dve, 1)
                        dve.wait_ge(gt_dve, n * GT + 5)
                        dve.wait_ge(gt_qb, n * 16 * H + 16 * H)
                        dve.tensor_tensor(q_all[:, :, :], q_all[:, :, :], wide_p, ALU.add).then_inc(gt_dve, 1)
                        dve.wait_ge(gt_dve, n * GT + 6)
                        dve.tensor_tensor(onehot[:, :, :], onehot[:, :, :], q_all[:, :, :],
                                          ALU.mult).then_inc(gt_dve, 1)
                        dve.wait_ge(gt_dve, n * GT + 7)
                        dve.tensor_reduce(extra, onehot[:, :, :], AX.X, ALU.add).then_inc(gt_dve, 1)
                        dve.tensor_scalar(wrapped, types, 0.0, None, ALU.not_equal).then_inc(gt_dve, 1)
                        dve.wait_ge(gt_dve, n * GT + 9)
                        dve.tensor_tensor(extra, extra, wrapped, ALU.mult).then_inc(gt_dve, 1)
                        dve.wait_ge(gt_dve, n * GT + 10)
                        dve.tensor_tensor(bias, bias, extra, ALU.add).then_inc(gt_dve, 1)
                        dve.wait_ge(gt_dve, n * GT + 11)

            def turn_x(i, o):
                g, s = group(i, o), o % 2
                dve.wait_ge(x_loaded, 16 * Q * (g + 1))
                if o >= 2:
                    dve.wait_ge(score_done, g - 1)
                for k in range(K):
                    dve.transpose(xT[:, s, k, :].rearrange("p (m b) -> p m b", b=B),
                                  x_in[:, :, :].rearrange("p m (a k) -> p k m a", k=K)[:, k, :, :]
                                  ).then_inc(xT_ready, 1)

            def x_low(i, o, k):
                dve.wait_ge(xT_hi_ready, K * group(i, o) + k + 1)
                dve.tensor_tensor(xT_lo[:, k, :], xT[:, o % 2, k, :], xT_hi[:, k, :],
                                  ALU.subtract).then_inc(xT_lo_ready, 1)

            def turn_probs(i, o):
                g = group(i, o)
                dve.wait_ge(prob_ready, g + 1)
                if o >= 1:
                    dve.wait_ge(agg_done, K * g)
                else:
                    dve.wait_ge(zeroed, 4)
                for q in range(Q):
                    for n in range(S // B):
                        first = q * B // S * S + n * B
                        dve.transpose(probT[first:first + B, :, quadrant(q)],
                                      prob[quadrant(q), :, n * B:(n + 1) * B]).then_inc(probT_ready, 1)

            def score_offsets(i, o):
                g = group(i, o)
                dve.wait_ge(xw_ready, T * (g + 1))
                if o >= 1:
                    dve.wait_ge(soft, SOFT * g)
                dve.scalar_tensor_tensor(out=offset[:, :, :], in0=adj_sb[:, ds(T * g, T), :], scalar=0.0,
                                         in1=xw[:, :, D:D + 1].broadcast_to((P, T, S)),
                                         op0=ALU.not_equal, op1=ALU.mult).then_inc(soft, 1)
                dve.wait_ge(soft, SOFT * g + 1)
                dve.tensor_tensor(offset[:, :, :], offset[:, :, :], bias_sb[:, ds(T * g, T), :],
                                  ALU.add).then_inc(soft, 1)

            def softmax_scores(i, o):
                g = group(i, o)
                dve.wait_ge(score_done, g + 1)
                if o >= 1:
                    dve.wait_ge(prob_ready, g)
                for h in range(H):
                    rows = slice(h * S, (h + 1) * S)
                    src = ps_score[rows, :].rearrange("p (t r) -> p t r", t=T)[:, :, rows]
                    dve.scalar_tensor_tensor(out=score[rows, :, :], in0=adj_sb[rows, ds(T * g, T), :],
                                             scalar=0.0, in1=src, op0=ALU.not_equal,
                                             op1=ALU.mult).then_inc(soft, 1)
                dve.wait_ge(soft, SOFT * g + H + 2)
                dve.tensor_tensor(score[:, :, :], score[:, :, :], offset[:, :, :],
                                  ALU.add).then_inc(soft, 1)
                dve.wait_ge(soft, SOFT * g + H + 3)
                dve.tensor_reduce(row_max[:, :], score[:, :, :], AX.X, ALU.max).then_inc(soft, 1)
                dve.wait_ge(soft, SOFT * g + H + 4)
                dve.tensor_tensor(score[:, :, :], score[:, :, :],
                                  row_max[:, :].unsqueeze(2).broadcast_to((P, T, S)),
                                  ALU.subtract).then_inc(soft, 1)

            def softmax_sums(i, o):
                g = group(i, o)
                dve.wait_ge(prob_ready, g + 1)
                dve.tensor_reduce(row_sum[:, :], prob[:, :, :], AX.X, ALU.add).then_inc(norm_ready, 1)
                dve.wait_ge(norm_ready, 2 * g + 1)
                dve.reciprocal(inv_sum[:, o % 2, :], row_sum[:, :]).then_inc(norm_ready, 1)

            def add_residual(i, o, t):
                s, g = o % 2, group(i, o)
                dve.wait_ge(out_done, T * g + t + 1)
                if t == 0:
                    dve.wait_ge(x_res_ready, g + 1)
                    dve.wait_ge(norm_ready, 2 * g + 2)
                    if o >= 1:
                        dve.wait_ge(out_stored[s], 16 * (i + o // 2))
                dve.scalar_tensor_tensor(out=y[:, s, t, :], in0=turn[t][:, 0:D],
                                         scalar=inv_sum[:, s, t:t + 1], in1=x_res[:, s, t, :],
                                         op0=ALU.mult, op1=ALU.add).then_inc(y_ready, 1)

            def tile_stats(i, o, t):
                g = group(i, o)
                dve.wait_ge(y_ready, T * g + t + 1)
                if t == 0 and o >= 1:
                    dve.wait_ge(mv_ready, T * g)
                dve.bn_stats(stats[:, t, :], y[:, o % 2, t, :]).then_inc(stats_ready, 1)

            def mean_variance(i, o):
                s, g = o % 2, group(i, o)
                dve.wait_ge(stats_ready, T * g + T)
                if o >= 1:
                    dve.wait_ge(ln_step, 3 * g)
                dve.sem_inc(dve_held, 1)
                for t in range(T):
                    dve.bn_aggr(mean_var[:, s, t, :], stats[:, t, :]).then_inc(mv_ready, 1)
                dve.wait_ge(mv_ready, T * g + T)
                dve.tensor_scalar(var_eps[:, :], mean_var[:, s, :, 1], EPS, None,
                                  ALU.add).then_inc(var_ready, 1)

            def last_group(o):
                s = o % 2

                def aggregate_stats(t):
                    if t == 0:
                        dve.wait_ge(ln_step, 3 * o)
                    dve.wait_ge(stats_ready, T * o + t + 1)
                    dve.bn_aggr(mean_var[:, s, t, :], stats[:, t, :]).then_inc(mv_ready, 1)

                def variance(t):
                    dve.wait_ge(mv_ready, T * o + t + 1)
                    dve.tensor_scalar(var_eps[:, t:t + 1], mean_var[:, s, t, 1:2], EPS, None,
                                      ALU.add).then_inc(var_ready, 1)

                def normalise(t):
                    dve.wait_ge(ln_step, 3 * (o + t) + 1)
                    dve.tensor_scalar(y[:, s, t, :], y[:, s, t, :], mean_var[:, s, t, 0:1],
                                      rstd[:, s, t:t + 1], ALU.subtract, ALU.mult).then_inc(last_ready, 1)

                for t in range(T + 1):
                    if t < T:
                        add_residual(0, o, t)
                    if t >= 1:
                        aggregate_stats(t - 1)
                    if t < T:
                        tile_stats(0, o, t)
                    if t >= 1:
                        variance(t - 1)
                normalise(T - 1)

            def h_low(i, o, c):
                dve.wait_ge(h_hi_ready, K * group(i, o) + c + 1)
                dve.scalar_tensor_tensor(out=h_lo[:, c, :], in0=wide[c][:, :], scalar=0.0,
                                         in1=h_hi[:, c, :], op0=ALU.max,
                                         op1=ALU.subtract).then_inc(h_lo_ready, 1)

            def step(i, o):
                g = group(i, o)
                more, before = o < GROUPS - 1, o >= 1
                if more and o > 0:
                    turn_x(i, o + 1)
                for t in range(T):
                    dve.wait_ge(xw_done, T * g + t + 1)
                    dve.tensor_tensor(xw[:, t, 0:D + 1], turn[t][:, 0:D + 1], xw_bias[:, :],
                                      ALU.add).then_inc(xw_ready, 1)
                    if o == 0:
                        if t == T - 2:
                            edge_flag()
                        edge_bias(bias_pieces[t])
                if o == 0:
                    dve.wait_ge(bias_ready, PIECES)
                    general_path()
                    turn_x(i, 1)
                    x_low(i, 1, 0)
                score_offsets(i, o)
                if o == 0:
                    for k in range(1, K):
                        x_low(i, 1, k)
                softmax_scores(i, o)
                if more and o > 0:
                    x_low(i, o + 1, 0)
                turn_probs(i, o)
                if more and o > 0:
                    x_low(i, o + 1, 1)
                    x_low(i, o + 1, 2)
                if o == 0:
                    wo_low()
                if o < GROUPS - 1:
                    if before:
                        for t in range(T - 1):
                            add_residual(i, o - 1, t)
                    h_low(i, o, 0)
                    if before:
                        add_residual(i, o - 1, T - 1)
                    for c in range(1, K):
                        h_low(i, o, c)
                    softmax_sums(i, o)
                    if before:
                        for t in range(T):
                            tile_stats(i, o - 1, t)
                        mean_variance(i, o - 1)
                else:
                    softmax_sums(i, o)
                    for t in range(T - 1):
                        add_residual(i, o - 1, t)
                        if t == 0:
                            tile_stats(i, o - 1, t)
                    h_low(i, o, 0)
                    tile_stats(i, o - 1, 1)
                    h_low(i, o, 1)
                    h_low(i, o, 2)
                    add_residual(i, o - 1, T - 1)
                    for t in range(2, T):
                        tile_stats(i, o - 1, t)
                    mean_variance(i, o - 1)

            dve.memset(ones[:, :], 1.0).then_inc(ones_ready, 1)
            dve.memset(embT[DEP:DEP + 1, :], 1.0).then_inc(zeroed, 1)
            dve.memset(probT[:, :, :], 0.0).then_inc(zeroed, 1)
            dve.memset(gw_hi[:, :, D:XC].bitcast(F32), 0.0).then_inc(zeroed, 1)
            dve.memset(gw_lo[:, :, D:XC].bitcast(F32), 0.0).then_inc(zeroed, 1)
            for c in (0, K - 1):
                dve.wait_ge(turned_w, K + c + 1)
                dve.tensor_copy(w2_e[:, c, :], turn[c][:, 0:D]).then_inc(w_e_dve, 1)
            turn_x(0, 0)
            for k in range(K):
                x_low(0, 0, k)
            b1_all, b2_all = ps_score[:, 0:D], turn[K][:, 0:D]
            sums = [(w2_d[:, k, :], b1_all, u_col[:, k:k + 1]) for k in range(K)]
            sums += [(w1_d[:, k, :], b2_all, w_col[:, k:k + 1]) for k in range(K)]
            for n, (rows, b_all, total) in enumerate(sums):
                if n < K:
                    g_low(n)
                if n == 0:
                    dve.wait_ge(dep_done, 1)
                if n == K:
                    gw_low()
                dve.tensor_tensor_reduce(y[:, n // T, n % T, :], rows, b_all, 1.0, 0.0, ALU.mult, ALU.add,
                                         total).then_inc(uwc_ready, 1)
            dve.tensor_copy(y[:, 1, T - 2, :], b2_all).then_inc(b2_copied, 1)
            dve.wait_ge(b2_copied, 1)
            dve.tensor_tensor_reduce(y[:, 1, T - 1, :], y[:, 1, T - 2, :], b1_all, 1.0, 0.0, ALU.mult, ALU.add,
                                     xw_bias[:, D:D + 1]).then_inc(uwc_ready, 1)
            w_low()
            steps(dve, step)
            last_group(GROUPS - 1)

        @block.tensor
        def _(pe):
            def warm_up(count):
                for _ in range(count):
                    pe.matmul(ps_score[:, 0:P], ones[:, :], ones[:, :], start=True, stop=True)

            pe.wait_ge(ones_ready, 1)
            warm_up(WARM[0])
            pe.wait_ge(const_ready, 2)
            for k in range(K):
                pe.wait_ge(w1_loaded[k], 16)
                for c in range(K):
                    mm = pe.transpose(wide[c][:, k * P:(k + 1) * P], w1_d[:, k, c * P:(c + 1) * P],
                                      ident[:, :])
                    if k == K - 1:
                        mm.then_inc(turned_w, 1)
            warm_up(WARM[1])
            pe.wait_ge(w2_loaded, 16)
            for c in range(K):
                for k in range(K):
                    mm = pe.transpose(turn[c][:, k * P:(k + 1) * P], w2_d[:, k, c * P:(c + 1) * P],
                                      ident[:, :])
                mm.then_inc(turned_w, 1)

            pe.wait_ge(emb_loaded, 16)
            pe.transpose(turn[K][0:DEP, P:P + NT], emb_sb[:, :], ident[0:NT, 0:NT]).then_inc(turned_emb, 1)

            def biases():
                pe.wait_ge(dep_loaded, 64)
                pe.wait_ge(embT_ready, 1)
                pe.wait_ge(zeroed, 1)
                for dst, w in ((ps_score, w1_dep), (turn[K], w2_dep)):
                    mm = pe.matmul(dst[:, 0:D], embT[:, 1:2].broadcast_to((DEP + 1, P)), w[:, :],
                                   start=True, stop=True)
                mm.then_inc(dep_done, 1)

            def g_rows(k):
                for c in range(K):
                    mm = pe.matmul(wide[k][:, 0:D], w1_e[:, c, k * P:(k + 1) * P], w2_e[:, c, :],
                                   start=(c == 0), stop=(c == K - 1))
                mm.then_inc(g_done, 1)

            def edge_test():
                pe.wait_ge(squared, PIECES)
                pe.wait_ge(uwc_ready, 2 * K + 1)
                pe.matmul(ps_score[0:1, 0:PIECES], ones[:, 0:1], flag_part[:, :],
                          start=True, stop=True).then_inc(flag_sum, 1)

            def general_path():
                pe.wait_ge(flag_ready, 1)
                other_types = pe.value_load(flag[0:1, 0:1], min_val=0, max_val=1)
                with pe.If(other_types > 0):
                    pe.wait_ge(yT_ready, K)
                    for n, w in enumerate((w1_dep, w2_dep)):
                        for c in range(K):
                            mm = pe.matmul(wide[n][:, c * NT:(c + 1) * NT], w[:, c * P:(c + 1) * P],
                                           embT[:, :], start=True, stop=True)
                    mm.then_inc(ge_pe, 1)
                    pe.wait_ge(ge_dve, 6)
                    for n, (w, d) in enumerate(((w1_e, d2T), (w2_e, d1T))):
                        for k in range(K):
                            for c in range(K):
                                pe.matmul(ps_score[:, (2 * k + n) * NT:(2 * k + n + 1) * NT],
                                          w[:, c, k * P:(k + 1) * P], d[:, c, :],
                                          start=(c == 0), stop=(c == K - 1))
                    for c in range(K):
                        pe.matmul(turn[K][0:1, 0:NT], bp[:, c, 0:1], d2T[:, c, :],
                                  start=(c == 0), stop=(c == K - 1))
                    for c in range(K):
                        mm = pe.matmul(turn[K][0:1, NT:2 * NT], ones[:, 0:1], dd[:, c, :],
                                       start=(c == 0), stop=(c == K - 1))
                    mm.then_inc(ge_pe, 1)
                    pe.wait_ge(ge_act, 2)
                    with pe.Fori(0, TILES) as k:
                        n = pe.snap(k)
                        pe.wait_ge(gt_x, n * 16 + 16)
                        features = lambda c: xg[:, :].rearrange("r (p k) -> r k p", k=K)[:, c, :]
                        for c in range(K):
                            mm = pe.transpose(wide[0][:, c * P:(c + 1) * P], features(c),
                                              ident[:, :])
                        mm.then_inc(gt_pe, 1)
                        pe.wait_ge(gt_act, n * 2 + 1)
                        for c in range(K):
                            pe.matmul(wide[1][:, 0:2 * NT], xgT[:, c, :], uv[:, c, :],
                                      start=(c == 0), stop=False)
                        pe.matmul(wide[1][:, 0:2 * NT], ones[0:1, :], pq_row[:, :], start=False,
                                  stop=True).then_inc(gt_pe, 1)
                    pe.wait_ge(gt_act, 2 * TILES)

            def three_passes(dst, k, pairs):
                for n, (lhs, rhs) in enumerate(pairs):
                    mm = pe.matmul(dst, lhs, rhs, start=(k == 0 and n == 0), stop=(k == K - 1 and n == 2))
                return mm

            def in_turn(count, early):
                order = [(n, k) for k in range(K - 1) for n in range(early)]
                order += [(n, K - 1) for n in range(early)]
                return order + [(n, k) for n in range(early, count) for k in range(K)]

            def y_product(i, o):
                g = group(i, o)
                for c, k in in_turn(K, 2 if o <= 1 else 1):
                    if c == 0:
                        pe.wait_ge(xT_lo_ready, K * g + k + 1)
                        if o == 0:
                            pe.wait_ge(g_lo_ready, k + 1)
                    if k == 0:
                        if o == 0:
                            pe.wait_ge(g_lo_ready, c + 1)
                        elif o == 1:
                            pe.wait_ge(yT_ready, c + 1)
                        else:
                            pe.wait_ge(h_lo_ready, K * (g - 1) + c + 1)
                    cols = slice(c * P, (c + 1) * P)
                    mm = three_passes(wide[c][:, :], k, (
                        (g_hi[:, k, cols], xT_hi[:, k, :]), (g_hi[:, k, cols], xT_lo[:, k, :]),
                        (g_lo[:, k, cols], xT_hi[:, k, :])))
                    if k == K - 1:
                        mm.then_inc(y_done, 1)

            def xw_product(i, o):
                g = group(i, o)
                if o == 0:
                    pe.wait_ge(gw_ready, 2)
                for t in range(T):
                    if o >= 2:
                        pe.wait_ge(y_ready, T * (g - 2) + t + 1)
                    elif o == 1:
                        pe.wait_ge(xw_ready, t + 1)
                    rows = slice(t * P, (t + 1) * P)
                    for k in range(K):
                        mm = three_passes(turn[t][:, 0:XC], k, (
                            (xT_hi[:, k, rows], gw_hi[:, k, :]), (xT_hi[:, k, rows], gw_lo[:, k, :]),
                            (xT_lo[:, k, rows], gw_hi[:, k, :])))
                    mm.then_inc(xw_done, 1)
                    if o == 0 and t == T - 2:
                        edge_test()

            def scores(i, o):
                g = group(i, o)
                pe.wait_ge(yT_ready, K * (g + 1))
                if o >= 1:
                    pe.wait_ge(soft, SOFT * (g - 1) + H + 2)
                for t in range(T):
                    rows = slice(t * P, (t + 1) * P)
                    for k in range(K):
                        mm = pe.matmul(ps_score[:, rows], yT[:, k, rows], xT[:, o % 2, k, rows],
                                       start=(k == 0), stop=(k == K - 1))
                mm.then_inc(score_done, 1)

            def out_product(i, o):
                g = group(i, o)
                if o == 0:
                    pe.wait_ge(wo_ready, 1)
                for t, k in in_turn(T, 2 if o == GROUPS - 1 else 1):
                    if t == 0:
                        pe.wait_ge(h_lo_ready, K * g + k + 1)
                    if k == 0:
                        if o < GROUPS - 1:
                            pe.wait_ge(xw_ready, T * (g + 1) + t + 1)
                        else:
                            pe.wait_ge(y_ready, T * (g - 1) + t + 1)
                    rows = slice(t * P, (t + 1) * P)
                    mm = three_passes(turn[t][:, 0:D], k, (
                        (h_hi[:, k, rows], wo_hi[:, k, :]), (h_hi[:, k, rows], wo_lo[:, k, :]),
                        (h_lo[:, k, rows], wo_hi[:, k, :])))
                    if k == K - 1:
                        mm.then_inc(out_done, 1)

            def aggregate(i, o):
                g = group(i, o)
                pe.wait_ge(probT_ready, PB * (g + 1))
                pe.wait_ge(xw_ready, T * (g + 1))
                if o == 0:
                    pe.wait_ge(zeroed, 4)
                for c in range(K):
                    if o == 0:
                        pe.wait_ge(yT_ready, K + c + 1)
                    for t in range(T):
                        mm = pe.matmul(wide[c][:, t * P:(t + 1) * P], xw[:, t, c * P:(c + 1) * P],
                                       probT[:, t, :], start=True, stop=True)
                    mm.then_inc(agg_done, 1)

            def step(i, o):
                if o != 1:
                    y_product(i, o)
                xw_product(i, o)
                if o == 0:
                    general_path()
                scores(i, o)
                if o >= 1:
                    out_product(i, o - 1)
                else:
                    y_product(i, 1)
                aggregate(i, o)

            warm_up(WARM[2])
            pe.wait_ge(w_e_act, K + 1)
            pe.wait_ge(w_e_dve, K - 1)
            for k in range(K):
                g_rows(k)
                if k == 0:
                    biases()
            steps(pe, step)
            out_product(0, GROUPS - 1)


INPUTS = ("x", "adj", "L0_gnn_dep_emb_table", "L0_gnn_W1_w", "L0_gnn_W1_b", "L0_gnn_W2_w", "L0_gnn_W2_b",
          "L0_gnn_gcn_w", "L0_gnn_gcn_b", "L0_gnn_Wo_w", "L0_gnn_Wo_b")


def kernel(**inputs):
    import concourse.bacc as bacc
    from concourse.bass_utils import run_bass_kernel_spmd

    nc = bacc.Bacc("TRN2", target_bir_lowering=False, num_devices=1)
    arrays, args = {}, []
    for name in INPUTS:
        a = np.ascontiguousarray(inputs[name])
        arrays[f"in_{name}"] = a
        args.append(nc.dram_tensor(f"in_{name}", a.shape, mybir.dt.from_np(a.dtype), kind="ExternalInput").ap())
    shape = arrays["in_x"].shape
    args.append(nc.dram_tensor("out_0", shape, F32, kind="ExternalOutput").ap())
    build(nc, *args)
    r = run_bass_kernel_spmd(nc, [arrays], core_ids=[0])
    return r.results[0]["out_0"]
```
